# Optimizing a Trainium2 kernel written in Bass

```python
import numpy as np
import jax
import jax.numpy as jnp

def _softmax(x, axis=-1):
    return jax.nn.softmax(x, axis=axis)

def _gelu(x):
    return jax.nn.gelu(x, approximate=True)

def _silu(x):
    return jax.nn.silu(x)

def _sigmoid(x):
    return jax.nn.sigmoid(x)

def _layernorm(x, axis=-1, eps=1e-05):
    m = jnp.mean(x, axis=axis, keepdims=True)
    v = jnp.var(x, axis=axis, keepdims=True)
    return (x - m) / jnp.sqrt(v + eps)

def _scatter_add(tgt, idx, src, axis=0):
    return tgt.at[idx].add(src)

def _segment_sum(src, seg, n):
    return jax.ops.segment_sum(src, seg, n)
kernel_name = 'mk_flamingo_gated_d1_seqx_r8_1c1614'

def setup_inputs(seed: int=0):
    np.random.seed(seed)
    _w = jnp.asarray

    def _rec_inputs():
        import jax
        import jax.numpy as jnp
        _rk = jax.random.key(seed)
        x = -0.0003929 + 0.9999 * jax.random.normal(jax.random.fold_in(_rk, 1), (64, 128, 128), jnp.float32)
        _lenS = 128 - jax.random.randint(jax.random.fold_in(_rk, 7), (64,), 0, max(1, 128 // 4) + 1, jnp.int32)
        _lenS2 = 77 - jax.random.randint(jax.random.fold_in(_rk, 8), (64,), 0, max(1, 77 // 4) + 1, jnp.int32)
        _ctx_512P = jax.random.normal(jax.random.fold_in(_rk, 11), (64, 16, 64), jnp.float32)
        _ctx_512c = jax.random.dirichlet(jax.random.fold_in(_rk, 511), 0.3 * jnp.ones((16,), jnp.float32), (64, 77))
        _ctx_512t = jnp.einsum('bsk,bkd->bsd', _ctx_512c, _ctx_512P)
        _ctx_512t = _ctx_512t * jax.lax.rsqrt(jnp.mean(jnp.square(_ctx_512t)) + 1e-12) * 0.953939
        ctx_512 = -1.39393e-06 + 0.999914 * (_ctx_512t + 0.3 * jax.random.normal(jax.random.fold_in(_rk, 611), (64, 77, 64), jnp.float32))
        _g = jax.random.normal(jax.random.fold_in(_rk, 9001), (2, 1), jnp.float32)
        _g = jnp.sign(_g) * jnp.maximum(jnp.abs(_g), 1.0) + (_g == 0) * 1.0
        g_xattn = _g[0]
        g_ffn = _g[1]
        return (x, ctx_512, g_xattn, g_ffn)
    x, ctx_512, g_xattn, g_ffn = _rec_inputs()

    def _L0_xattn_setup():
        import jax, jax.numpy as jnp
        import numpy as np
        HEADS = 16
        D_MODEL = 128
        IMG_MODEL = 64
        D_K = D_MODEL // HEADS
        key = jax.random.key(seed)
        ks = jax.random.split(key, 12)
        B, LQ, LKV = (8, 256, 128)
        s_dm = 1.0 / np.sqrt(D_MODEL)
        s_im = 1.0 / np.sqrt(IMG_MODEL)
        return {'q': jax.random.normal(ks[0], (B, LQ, D_MODEL), jnp.float32), 'k': jax.random.normal(ks[1], (B, LKV, IMG_MODEL), jnp.float32), 'v': jax.random.normal(ks[2], (B, LKV, IMG_MODEL), jnp.float32), 'Wq': jax.random.normal(ks[3], (D_MODEL, D_MODEL), jnp.float32) * s_dm, 'bq': jnp.zeros((D_MODEL,), jnp.float32), 'Wk': jax.random.normal(ks[4], (IMG_MODEL, D_MODEL), jnp.float32) * s_im, 'bk': jnp.zeros((D_MODEL,), jnp.float32), 'Wv': jax.random.normal(ks[5], (IMG_MODEL, D_MODEL), jnp.float32) * s_im, 'bv': jnp.zeros((D_MODEL,), jnp.float32), 'Wo': jax.random.normal(ks[6], (D_MODEL, D_MODEL), jnp.float32) * s_dm, 'bo': jnp.zeros((D_MODEL,), jnp.float32)}
    _L0_xattn_all = _L0_xattn_setup()
    _L0_xattn_in = {k: v for k, v in _L0_xattn_all.items() if k in ('Wq', 'bq', 'Wk', 'bk', 'Wv', 'bv', 'Wo', 'bo')}
    del _L0_xattn_all

    def _L0_ffn_setup():
        import jax, jax.numpy as jnp
        import numpy as np
        N_EMBED = 128
        FFN_HIDDEN = 512
        NUM_EXPERTS = 8
        TOP_K = 2
        key = jax.random.key(seed)
        ks = jax.random.split(key, 8)
        d, f, E = (N_EMBED, FFN_HIDDEN, NUM_EXPERTS)
        s_d = 1.0 / np.sqrt(d)
        s_f = 1.0 / np.sqrt(f)
        return {'x': jax.random.normal(ks[0], (2, 256, d), dtype=jnp.float32), 'Wg': jax.random.uniform(ks[1], (d, E), jnp.float32, -s_d, s_d), 'bg': jax.random.uniform(ks[2], (E,), jnp.float32, -s_d, s_d), 'W1': jax.random.uniform(ks[3], (E, d, f), jnp.float32, -s_d, s_d), 'b1': jax.random.uniform(ks[4], (E, f), jnp.float32, -s_d, s_d), 'W2': jax.random.uniform(ks[5], (E, f, d), jnp.float32, -s_f, s_f), 'b2': jax.random.uniform(ks[6], (E, d), jnp.float32, -s_f, s_f)}
    _L0_ffn_all = _L0_ffn_setup()
    _L0_ffn_in = {k: v for k, v in _L0_ffn_all.items() if k in ('Wg', 'bg', 'W1', 'b1', 'W2', 'b2')}
    del _L0_ffn_all
    return {'x': x, 'ctx_512': ctx_512, 'g_xattn': g_xattn, 'g_ffn': g_ffn, 'L0_xattn_Wq': _L0_xattn_in['Wq'], 'L0_xattn_bq': _L0_xattn_in['bq'], 'L0_xattn_Wk': _L0_xattn_in['Wk'], 'L0_xattn_bk': _L0_xattn_in['bk'], 'L0_xattn_Wv': _L0_xattn_in['Wv'], 'L0_xattn_bv': _L0_xattn_in['bv'], 'L0_xattn_Wo': _L0_xattn_in['Wo'], 'L0_xattn_bo': _L0_xattn_in['bo'], 'L0_ffn_Wg': _L0_ffn_in['Wg'], 'L0_ffn_bg': _L0_ffn_in['bg'], 'L0_ffn_W1': _L0_ffn_in['W1'], 'L0_ffn_b1': _L0_ffn_in['b1'], 'L0_ffn_W2': _L0_ffn_in['W2'], 'L0_ffn_b2': _L0_ffn_in['b2']}

def reference(x, ctx_512, g_xattn, g_ffn, L0_xattn_Wq, L0_xattn_bq, L0_xattn_Wk, L0_xattn_bk, L0_xattn_Wv, L0_xattn_bv, L0_xattn_Wo, L0_xattn_bo, L0_ffn_Wg, L0_ffn_bg, L0_ffn_W1, L0_ffn_b1, L0_ffn_W2, L0_ffn_b2):
    import jax
    import jax.numpy as jnp

    def _L0_xattn_ref(q, k, v, Wq, bq, Wk, bk, Wv, bv, Wo, bo):
        import jax, jax.numpy as jnp
        import numpy as np
        HEADS = 16
        D_MODEL = 128
        IMG_MODEL = 64
        D_K = D_MODEL // HEADS
        B, LQ, _ = q.shape
        LKV = k.shape[1]
        qh = (q @ Wq + bq).reshape(B, LQ, HEADS, D_K).transpose(0, 2, 1, 3)
        kh = (k @ Wk + bk).reshape(B, LKV, HEADS, D_K).transpose(0, 2, 1, 3)
        vh = (v @ Wv + bv).reshape(B, LKV, HEADS, D_K).transpose(0, 2, 1, 3)
        scale = 1.0 / np.sqrt(D_K)
        scores = jnp.einsum('bhqd,bhkd->bhqk', qh, kh) * scale
        attn = jax.nn.softmax(scores, axis=-1)
        out = jnp.einsum('bhqk,bhkd->bhqd', attn, vh)
        concat = out.transpose(0, 2, 1, 3).reshape(B, LQ, D_MODEL)
        return concat @ Wo + bo

    def _L0_ffn_ref(x, Wg, bg, W1, b1, W2, b2):
        import jax, jax.numpy as jnp
        import numpy as np
        N_EMBED = 128
        FFN_HIDDEN = 512
        NUM_EXPERTS = 8
        TOP_K = 2
        gate_scores = jax.nn.softmax(x @ Wg + bg, axis=-1)
        topk_scores, topk_idx = jax.lax.top_k(gate_scores, TOP_K)
        topk_scores = topk_scores / (jnp.sum(topk_scores, axis=-1, keepdims=True) + 1e-08)
        onehot = jax.nn.one_hot(topk_idx, NUM_EXPERTS, dtype=x.dtype)
        combine_w = jnp.einsum('bsk,bske->bse', topk_scores, onehot)
        output = jnp.zeros_like(x)
        for e in range(NUM_EXPERTS):
            h = jax.nn.gelu(x @ W1[e] + b1[e])
            y = h @ W2[e] + b2[e]
            output = output + y * combine_w[..., e:e + 1]
        return output
    x = x + jnp.tanh(g_xattn[0]) * _L0_xattn_ref(_layernorm(x, axis=-1), ctx_512, ctx_512, L0_xattn_Wq, L0_xattn_bq, L0_xattn_Wk, L0_xattn_bk, L0_xattn_Wv, L0_xattn_bv, L0_xattn_Wo, L0_xattn_bo)
    x = x + jnp.tanh(g_ffn[0]) * _L0_ffn_ref(_layernorm(x, axis=-1), L0_ffn_Wg, L0_ffn_bg, L0_ffn_W1, L0_ffn_b1, L0_ffn_W2, L0_ffn_b2)
    return x

_drawn_inputs = setup_inputs


def setup_inputs(seed=0):
    import zlib

    import numpy as np

    out = dict(_drawn_inputs(seed))
    spreads = {'L0_xattn_bq': (0.0, 0.307),
     'L0_xattn_bk': (0.0, 0.8),
     'L0_xattn_bv': (0.0, 0.1),
     'L0_xattn_bo': (0.0, 0.1)}
    factors = {'L0_ffn_b1': 4.892, 'L0_ffn_b2': 3.505}
    for name, (base, spread) in spreads.items():
        noise = np.random.default_rng([zlib.crc32(name.encode()), seed]).standard_normal(out[name].shape)
        drawn = base * np.exp(spread * noise) if base else spread * noise
        out[name] = jnp.asarray(drawn.astype(out[name].dtype))
    for name, factor in factors.items():
        out[name] = (out[name] * factor).astype(out[name].dtype)
    return out
```

```python
from contextlib import ExitStack

import concourse.bass as bass
from concourse import mybir

F32 = mybir.dt.float32
F32R = mybir.dt.float32r
F16 = mybir.dt.float16
BF16 = mybir.dt.bfloat16
I32 = mybir.dt.int32
ALU = mybir.AluOpType
ACT = mybir.ActivationFunctionType
AX = mybir.AxisListType

HEADS = 16
DK = 8
EPS = 1e-5
GH = 4
TERMS = 3
ROWS = TERMS * GH * DK
VW = 27


def at(eng, sem, value):
    if not isinstance(value, int) or value > 0:
        eng.wait_ge(sem, value)


def flamingo(nc, x, ctx_in, g_xattn, g_ffn, Wq, bq, Wk, bk, Wv, bv, Wo, bo, Wg, bg, W1, b1, W2, b2, out, STAGE=9):
    B, T, D = x.shape
    KV, DC = ctx_in.shape[1:]
    NG = HEADS // GH
    CB = 4
    LOADS = 8
    XB = B // LOADS
    GW = GH * KV
    HALF = HEADS // 2
    SCALE = float(1.0 / (DK ** 0.5))

    E, _, F = W1.shape
    FC = F // 128
    TILE = 256
    SUB = TILE // 128
    TILES = 2 * B * T // TILE + E
    O_B1 = F
    O_W2 = F + FC
    O_B2 = O_W2 + FC * D
    BUNDLE = O_B2 + D

    es = ExitStack()
    with es:
        routed = nc.dram_tensor("routed", (TILES * TILE, D), F32, kind="Internal").ap()
        expert_out = nc.dram_tensor("expert_out", (TILES * TILE, D), F32, kind="Internal").ap()

        def sb(name, shape, dt=F32):
            return es.enter_context(nc.sbuf_tensor(name, shape, dt))

        def ps(name, shape, dt=F32):
            return es.enter_context(nc.psum_tensor(name, shape, dt))

        def sem(name):
            return es.enter_context(nc.semaphore(name))

        ident = sb("ident", [128, 128])
        neg_ident = sb("neg_ident", [128, 128], F32R)
        headmask = sb("headmask", [ROWS, GH])
        wq3 = sb("wq3", [D, NG, ROWS])
        bq3 = sb("bq3", [ROWS, NG])
        wk3 = sb("wk3", [DC + 1, NG, ROWS])
        wv = sb("wv", [DC + 1, D])
        wo = sb("wo", [D, D])
        bo_rows = sb("bo_rows", [T, D])
        gate = sb("gate", [128, 2])
        xs = sb("xs", [T, B, D])
        mean = sb("mean", [T, B, 2])
        rstd = sb("rstd", [T, B])
        half_power = sb("half_power", [T, B])
        early_ctx = sb("early_ctx", [128, B * KV])
        ctxT = early_ctx[0:DC + 1, :]
        arena = sb("arena", [128, max(B * HEADS * VW // 2, E * BUNDLE)])
        vparts = arena[0:KV, 0:B * HEADS * VW // 2].bitcast(BF16).rearrange("p (b c) -> p b c", b=B)
        experts = arena[:, 0:E * BUNDLE].rearrange("p (e c) -> p e c", e=E)
        ctx_rows = sb("ctx_rows", [KV, 2, CB, DC + 1])
        ctxT_now = sb("ctxT_now", [DC + 1, 2, CB * KV])
        v_rest = sb("v_rest", [KV, 2, CB * D])
        stats = sb("stats", [T, 4, 6])
        moments = sb("moments", [T, 4, 2])
        xn = sb("xn", [T, 2, D])
        xnT = sb("xnT", [D, 2, T])
        kst = sb("kst", [ROWS, 2, NG, KV], F32R)
        km = sb("km", [ROWS, 2, NG, GH, KV], F32R)
        qb = sb("qb", [ROWS, NG, T])
        qst = sb("qst", [ROWS, 2, NG, T], F32R)
        mx = sb("mx", [T, 2, HEADS], F32R)
        early_p = sb("early_p", [128, 2 * HEADS * T])
        p32 = early_p[0:KV, :].rearrange("p (u h q) -> p u h q", u=2, q=T)
        p1 = sb("p1", [KV, 2, HEADS, T], F16)
        p2 = sb("p2", [KV, 2, HEADS, T], F16)
        osum = sb("osum", [T, 2, HEADS, DK + 1])
        rden = sb("rden", [T, 2, HEADS])
        cc = sb("cc", [T, 2, D])
        ccT = sb("ccT", [D, 2, T])

        wg = sb("wg", [D, E])
        bg_rows = sb("bg_rows", [T, E])
        rank_e = sb("rank_e", [T, E])
        ones = sb("ones", [T, T], BF16)
        before = sb("before", [T, T], BF16)
        logits = sb("logits", [T, B, E])
        probs = sb("probs", [T, B, E])
        row_stat = sb("row_stat", [T, B])
        top = sb("top", [T, B, 2])
        onehot = sb("onehot", [T, B, 2, E])
        chosen = sb("chosen", [T, B, E], BF16)
        weight = sb("weight", [T, B, 2])
        scan = sb("scan", [T, 2, B, E])
        place = sb("place", [T, B, E])
        slot_f = sb("slot_f", [T, B, 2])
        slots = sb("slots", [T, B, 2], I32)
        ntile = sb("ntile", [T, E])
        ntile_i = sb("ntile_i", [T, E], I32)
        cum = sb("cum", [T, 2, E])
        first_row = sb("first_row", [T, E])
        tile_no = sb("tile_no", [1, TILES])
        reached = sb("reached", [1, TILES, E - 1])
        tile_f = sb("tile_f", [1, TILES])
        tile_expert = sb("tile_expert", [1, TILES], I32)
        zeros = sb("zeros", [128, SUB * D])
        slot_now = sb("slot_now", [T, 2, 2], I32)

        def part(space, start, *dims):
            size = 1
            for d in dims:
                size *= d
            view = space[:, start:start + size]
            if len(dims) == 2:
                return view.rearrange("p (a b) -> p a b", b=dims[1])
            return view.rearrange("p (a b c) -> p a b c", b=dims[1], c=dims[2])

        wbuf = part(early_ctx, 0, 2, BUNDLE)
        hT = part(early_ctx, 2 * BUNDLE, 2, FC, TILE)
        xg = part(early_p, 0, 2, SUB, D)
        xgT = part(early_p, 2 * TILE, 2, TILE)
        yb = part(early_p, 4 * TILE, 2, SUB, D)
        picked = part(early_p, 6 * TILE, 2, 2, D)
        result = part(early_p, 8 * TILE, 2, D)

        s_ps = ps("s_ps", [T, 2, 512])
        st_ps = ps("st_ps", [128, 2, 2, 512])
        av_ps = ps("av_ps", [T, 512])
        misc_ps = ps("misc_ps", [128, 512])

        const_made = sem("const_made")
        weights_in = sem("weights_in")
        x_in = [sem(f"x_in{i}") for i in range(LOADS)]
        ctx_in_u = [sem(f"ctx_in{u}") for u in range(2)]
        gates_done = sem("gates_done")
        wo_scaled = sem("wo_scaled")
        bo_scaled = sem("bo_scaled")
        mean_done = sem("mean_done")
        rstd_done = sem("rstd_done")
        ctxT_ps = sem("ctxT_ps")
        ctxT_sb = sem("ctxT_sb")
        v_ps = sem("v_ps")
        v1_done = sem("v1_done")
        v_chain = sem("v_chain")
        xn_done = sem("xn_done")
        xnT_ps = sem("xnT_ps")
        xnT_sb = sem("xnT_sb")
        k_ps = sem("k_ps")
        kh_done = sem("kh_done")
        k_done = sem("k_done")
        km_done = sem("km_done")
        q_ps = sem("q_ps")
        qb_done = sem("qb_done")
        qh_done = sem("qh_done")
        q_done = sem("q_done")
        s_done = sem("s_done")
        max_done = sem("max_done")
        st_done = sem("st_done")
        exp_done = sem("exp_done")
        p1_done = sem("p1_done")
        p2_done = sem("p2_done")
        av_done = sem("av_done")
        osum_done = sem("osum_done")
        rden_done = sem("rden_done")
        cc_done = sem("cc_done")
        ccT_ps = sem("ccT_ps")
        ccT_sb = sem("ccT_sb")
        proj_done = sem("proj_done")
        x2_done = sem("x2_done")
        xbo_done = sem("xbo_done")
        stored = sem("stored")
        chain = sem("chain")
        pool_passed = sem("pool_passed")
        dve_passed = sem("dve_passed")
        zeros_made = sem("zeros_made")
        wg_in = sem("wg_in")
        experts_in = sem("experts_in")
        stat2 = sem("stat2")
        rstd2 = sem("rstd2")
        xn2_done = sem("xn2_done")
        xn2T_ps = sem("xn2T_ps")
        xn2T_sb = sem("xn2T_sb")
        gate_done = sem("gate_done")
        logits_done = sem("logits_done")
        gate_exp = sem("gate_exp")
        chosen_done = sem("chosen_done")
        count_done = sem("count_done")
        table_done = sem("table_done")
        row_done = sem("row_done")
        scattered = [sem(f"scattered{u}") for u in range(2)]
        cleared = sem("cleared")
        xg_in = [sem(f"xg_in{u}") for u in range(2)]
        w1_done = sem("w1_done")
        w2_done = sem("w2_done")
        xgT_ps = sem("xgT_ps")
        xgT_sb = sem("xgT_sb")
        h_ps = sem("h_ps")
        h_sb = sem("h_sb")
        y_ps = sem("y_ps")
        y_done = sem("y_done")
        y_out = [sem(f"y_out{u}") for u in range(2)]
        slot_done = sem("slot_done")
        gathered = [sem(f"gathered{u}") for u in range(2)]
        res_chain = sem("res_chain")
        res_done = sem("res_done")
        res_out = [sem(f"res_out{u}") for u in range(2)]

        block = es.enter_context(nc.Block())
        ALL_CONSTS = 9 + 2 * TERMS + 3
        LAST = 4

        def steps(eng, step):
            for k in range(LAST):
                step(k, k % 2)
            with eng.Fori(0, (B - LAST) // 2) as i:
                for u in range(2):
                    step(i * 2 + (LAST + u), u)
            for k in range(B, B + LAST):
                step(k, k % 2)

        def tile_steps(eng, step):
            for k in range(4):
                step(k, k % 2)
            with eng.Fori(0, (TILES - 4) // 2) as i:
                for u in range(2):
                    step(i * 2 + (4 + u), u)
            for k in range(TILES, TILES + 2):
                step(k, k % 2)

        def has_tile(k, lag):
            return not isinstance(k, int) or 0 <= k - lag < TILES

        def has(k, lag):
            return not isinstance(k, int) or 0 <= k - lag < B

        @block.sync
        def _(sp):
            def load_ctx(c, u):
                if isinstance(c, int):
                    at(sp, const_made, 3)
                else:
                    sp.wait_ge(ctxT_ps, c - 1)
                src = ctx_in[c * CB:(c + 1) * CB] if isinstance(c, int) else ctx_in[bass.ds(c * CB, CB)]
                sp.dma_start(ctx_rows[:, u, :, 0:DC], src.rearrange("b p d -> p b d")).then_inc(ctx_in_u[u], 16)

            for t in range(TERMS):
                sp.dma_start(wq3[:, :, 32 * t:32 * t + 32],
                             Wq.rearrange("d (g i) -> d g i", g=NG)).then_inc(weights_in, 16)
                sp.dma_start(wk3[0:DC, :, 32 * t:32 * t + 32],
                             Wk.rearrange("d (g i) -> d g i", g=NG)).then_inc(weights_in, 16)
                sp.dma_start(wk3[DC:DC + 1, :, 32 * t:32 * t + 32],
                             bk.rearrange("(a g i) -> a g i", a=1, g=NG)).then_inc(weights_in, 16)
                with nc.allow_non_contiguous_dma("one bias row per partition"):
                    sp.dma_start(bq3[32 * t:32 * t + 32, :],
                                 bq.rearrange("(g i) -> i g", g=NG)).then_inc(weights_in, 16)
            sp.dma_start(wv[0:DC, :], Wv).then_inc(weights_in, 16)
            sp.dma_start(wv[DC:DC + 1, :], bv.rearrange("(a n) -> a n", a=1)).then_inc(weights_in, 16)
            for u in range(2):
                load_ctx(u, u)
            for n in range(LOADS):
                sp.dma_start(xs[:, n * XB:(n + 1) * XB, :],
                             x[n * XB:(n + 1) * XB].rearrange("b p d -> p b d")).then_inc(x_in[n], 16)
            with sp.Fori(0, B // CB // 2 - 1) as i:
                for u in range(2):
                    load_ctx(i * 2 + (u + 2), u)
            sp.wait_ge(zeros_made, 1)
            sp.dma_start(routed.rearrange("(i p s) d -> p i (s d)", p=128, s=SUB),
                         zeros[:, :].unsqueeze(1).broadcast_to([128, TILES, SUB * D])).then_inc(cleared, 16)
            if STAGE == 1:
                sp.wait_ge(x2_done, B)
                sp.dma_start(out.rearrange("b p d -> p b d"), xs[:, :, :]).then_inc(stored, 16)
                sp.wait_ge(stored, 16)

            sp.wait_ge(av_done, B)
            view = experts
            sp.dma_start(view[:, :, 0:F], W1.rearrange("e d f -> d e f")).then_inc(experts_in, 16)
            with nc.allow_non_contiguous_dma("one bias per partition"):
                for c in range(FC):
                    sp.dma_start(view[:, :, O_B1 + c], b1[:, c * 128:(c + 1) * 128].rearrange("e p -> p e")).then_inc(experts_in, 16)
            for c in range(FC):
                sp.dma_start(view[:, :, O_W2 + c * D:O_W2 + (c + 1) * D],
                             W2[:, c * 128:(c + 1) * 128, :].rearrange("e p d -> p e d")).then_inc(experts_in, 16)
            sp.dma_start(view[:, :, O_B2:BUNDLE], b2.partition_broadcast(128)).then_inc(experts_in, 16)
            for u in range(2):
                sp.wait_ge(scattered[u], 16 * B)

            def load_tile(i, u):
                if not isinstance(i, int):
                    sp.wait_ge(xgT_ps, i - 1)
                sp.dma_start(xg[:, u], routed[bass.ds(i * TILE, TILE), :].rearrange("(p s) d -> p s d", s=SUB)).then_inc(xg_in[u], 16)

            for u in range(2):
                load_tile(u, u)
            with sp.Fori(0, TILES // 2 - 1) as i:
                for u in range(2):
                    load_tile(i * 2 + (u + 2), u)

            with sp.Fori(0, B // 2) as i:
                for u in range(2):
                    b = i * 2 + u
                    sp.wait_ge(res_done, b + 1)
                    sp.dma_start(out[bass.ds(b, 1)].rearrange("a p d -> p (a d)"), result[:, u, :]).then_inc(res_out[u], 16)
            for u in range(2):
                sp.wait_ge(res_out[u], 16 * (B // 2))

        WEIGHT_LOADS = 16 * (4 * TERMS + 2)

        @block.gpsimd
        def _(pool):
            made = [0]

            def make(instruction):
                made[0] += 1
                instruction.then_inc(const_made, 1)
                pool.wait_ge(const_made, made[0])

            make(nc.gpsimd.memset(ident[:, :], 0.0))
            make(nc.gpsimd.affine_select(out=ident[:, :], in_=ident[:, :], compare_op=ALU.not_equal, fill=1.0,
                                         base=0, pattern=[[-1, 128]], channel_multiplier=1))
            make(nc.gpsimd.memset(ctx_rows[:, :, :, DC:DC + 1], 1.0))
            make(nc.gpsimd.memset(headmask[:, :], 1.0))
            for t in range(TERMS):
                rows = headmask[32 * t:32 * t + 32, :]
                make(nc.gpsimd.affine_select(out=rows, in_=rows, compare_op=ALU.is_ge, fill=0.0,
                                             base=0, pattern=[[-DK, GH]], channel_multiplier=1))
                make(nc.gpsimd.affine_select(out=rows, in_=rows, compare_op=ALU.is_ge, fill=0.0,
                                             base=DK - 1, pattern=[[DK, GH]], channel_multiplier=-1))
            make(nc.gpsimd.memset(half_power[:, :], -0.5))
            make(nc.gpsimd.memset(ones[:, :], 1.0))
            make(nc.gpsimd.affine_select(out=before[:, :], in_=ones[:, :], compare_op=ALU.is_gt, fill=0.0,
                                         base=0, pattern=[[1, T]], channel_multiplier=-1))
            make(nc.gpsimd.iota(rank_e[:, :], pattern=[[-1, E]], base=E, channel_multiplier=0,
                                allow_small_or_imprecise_dtypes=True))
            make(nc.gpsimd.iota(tile_no[:, :], pattern=[[1, TILES]], base=0, channel_multiplier=0,
                                allow_small_or_imprecise_dtypes=True))
            nc.gpsimd.memset(zeros[:, :], 0.0).then_inc(zeros_made, 1)
            vv = vparts.rearrange("p b (h c) -> p (b h) c", c=VW)
            make(nc.gpsimd.memset(vv[:, :, DK:DK + 1], 1.0))
            make(nc.gpsimd.memset(vv[:, :, 2 * DK + 1:2 * DK + 2], 0.0))
            make(nc.gpsimd.memset(vv[:, :, 3 * DK + 2:3 * DK + 3], 0.0))
            pool.wait_ge(mean_done, B // 4 * 9 + 1)
            nc.gpsimd.tensor_tensor(rstd[:, :], rstd[:, :], half_power[:, :], ALU.pow).then_inc(rstd_done, 1)

            def step(k, u):
                if has(k, 0):
                    pool.wait_ge(k_done, k + 1)
                    at(pool, st_done, 2 * k - 2)
                    nc.gpsimd.tensor_tensor(
                        km[:, u], kst[:, u].bitcast(F32).unsqueeze(2).broadcast_to([ROWS, NG, GH, KV]),
                        headmask[:, :].unsqueeze(1).unsqueeze(3).broadcast_to([ROWS, NG, GH, KV]),
                        ALU.mult).then_inc(km_done, 1)
                if has(k, 1):
                    b = k - 1
                    pool.wait_ge(xn_done, k)
                    if isinstance(k, int) and k == 1:
                        pool.wait_ge(bo_scaled, 1)
                    nc.gpsimd.tensor_tensor(xs[:, b, :], xs[:, b, :], bo_rows[:, :], ALU.add).then_inc(xbo_done, 1)

            steps(pool, step)

            pool.wait_ge(stat2, B // 4 * 9 + 1)
            nc.gpsimd.tensor_tensor(rstd[:, :], rstd[:, :], half_power[:, :], ALU.pow).then_inc(rstd2, 1)

            pool.wait_ge(cleared, 16)
            with pool.Fori(0, B // 2) as i:
                for u in range(2):
                    b = i * 2 + u
                    pool.wait_ge(row_done, b * 2 + 2)
                    nc.gpsimd.sem_inc(pool_passed)
                    for c in range(2):
                        nc.gpsimd.indirect_dma_start(
                            out=routed, out_offset=bass.IndirectOffsetOnAxis(ap=slot_now[:, u, c:c + 1], axis=0),
                            in_=xn[:, u, :], in_offset=None).then_inc(scattered[u], 16)

            def store_y(i, u):
                pool.wait_ge(y_done, i + 1)
                pool.dma_start(expert_out[bass.ds(i * TILE, TILE), :].rearrange("(p s) d -> p s d", s=SUB),
                               yb[:, u]).then_inc(y_out[u], 16)

            with pool.Fori(0, TILES // 2) as i:
                for u in range(2):
                    store_y(i * 2 + u, u)
            for u in range(2):
                pool.wait_ge(y_out[u], 16 * (TILES // 2))

            with pool.Fori(0, B // 2) as i:
                for u in range(2):
                    b = i * 2 + u
                    pool.wait_ge(slot_done, b + 1)
                    nc.gpsimd.sem_inc(pool_passed)
                    for c in range(2):
                        nc.gpsimd.indirect_dma_start(
                            out=picked[:, u, c, :], out_offset=None, in_=expert_out,
                            in_offset=bass.IndirectOffsetOnAxis(ap=slot_now[:, u, c:c + 1], axis=0)).then_inc(gathered[u], 16)

        @block.scalar
        def _(act):
            act.dma_start(wg[:, :], Wg).then_inc(wg_in, 16)
            act.dma_start(bg_rows[:, :], bg.partition_broadcast(T)).then_inc(wg_in, 16)
            act.dma_start(wo[:, :], Wo).then_inc(gates_done, 16)
            act.dma_start(bo_rows[:, :], bo.partition_broadcast(T)).then_inc(gates_done, 16)
            act.dma_start(gate[:, 0:1], g_xattn.partition_broadcast(128)).then_inc(gates_done, 16)
            act.dma_start(gate[:, 1:2], g_ffn.partition_broadcast(128)).then_inc(gates_done, 16)
            act.wait_ge(gates_done, 64)
            nc.scalar.activation(gate[:, :], gate[:, :], ACT.Tanh).then_inc(gates_done, 1)
            act.wait_ge(gates_done, 65)
            nc.scalar.activation(wo[:, :], wo[:, :], ACT.Copy, scale=gate[:, 0:1]).then_inc(wo_scaled, 1)
            nc.scalar.activation(bo_rows[:, :], bo_rows[:, :], ACT.Copy, scale=gate[:, 0:1]).then_inc(bo_scaled, 1)
            act.wait_ge(const_made, 2)
            nc.scalar.activation(neg_ident[:, :], ident[:, :], ACT.Copy, scale=-1.0).then_inc(wo_scaled, 1)

            with act.Fori(0, B // CB // 2) as i:
                for u in range(2):
                    c = i * 2 + u
                    act.wait_ge(ctxT_ps, c + 1)
                    src = misc_ps[0:DC + 1, 0:CB * KV] if u == 0 else av_ps[0:DC + 1, 0:CB * KV]
                    nc.scalar.activation(ctxT_now[:, u, :], src, ACT.Copy).then_inc(ctxT_sb, 1)
                    nc.scalar.activation(ctxT[:, bass.ds(c * (CB * KV), CB * KV)], src, ACT.Copy).then_inc(ctxT_sb, 1)
                    act.wait_ge(v_ps, c + 1)
                    nc.scalar.activation(
                        vparts[:, bass.ds(c * CB, CB), :].rearrange("p b (h c) -> p (b h) c", c=VW)[:, :, 0:DK],
                        st_ps[0:KV, u, 0, :].rearrange("p (h c) -> p h c", c=DK), ACT.Copy).then_inc(v1_done, 1)

            def step(k, u):
                def exp(half, dst, done):
                    b = k - 2
                    nc.scalar.activation(dst[:, u, half * HALF:(half + 1) * HALF, :],
                                         st_ps[0:KV, half, :, :].rearrange("p a (h q) -> p (a h) q", q=T),
                                         ACT.Exp, scale=SCALE).then_inc(done, 1)

                if has(k, 2):
                    act.wait_ge(st_done, 2 * k - 3)
                    at(act, p2_done, 2 * k - 6)
                    exp(0, p32, exp_done)
                if has(k, 0):
                    act.wait_ge(k_ps, k + 1)
                    at(act, km_done, k - 1)
                    nc.scalar.activation(kst[:, u], misc_ps[0:ROWS, 0:NG * KV].rearrange("p (g k) -> p g k", g=NG),
                                         ACT.Copy).then_inc(kh_done, 1)
                if has(k, 2):
                    at(act, av_done, k - 3)
                    exp(0, p1, p1_done)
                if has(k, 0):
                    act.wait_ge(xnT_ps, k + 1)
                    at(act, q_ps, k - 1)
                    nc.scalar.activation(xnT[:, u, :], misc_ps[:, 0:T], ACT.Copy).then_inc(xnT_sb, 1)
                if has(k, 2):
                    act.wait_ge(st_done, 2 * k - 2)
                    exp(1, p32, exp_done)
                if has(k, 0):
                    act.wait_ge(qb_done, k + 1)
                    at(act, st_done, 2 * k - 2)
                    nc.scalar.activation(qst[:, u], qb[:, :, :], ACT.Copy).then_inc(qh_done, 1)
                if has(k, 2):
                    exp(1, p1, p1_done)
                if has(k, 4):
                    act.wait_ge(ccT_ps, k - 3)
                    at(act, proj_done, k - 4)
                    nc.scalar.activation(ccT[:, u, :], misc_ps[:, 0:T], ACT.Copy).then_inc(ccT_sb, 1)

            steps(act, step)

            act.wait_ge(proj_done, B)
            with act.Fori(0, B // 2) as i:
                for u in range(2):
                    b = i * 2 + u
                    act.wait_ge(xn2T_ps, b + 1)
                    nc.scalar.activation(xnT[:, u, :], misc_ps[:, 0:T], ACT.Copy).then_inc(xn2T_sb, 1)
            act.wait_ge(logits_done, 1)
            nc.scalar.activation(probs[:, :, :], logits[:, :, :], ACT.Exp).then_inc(gate_exp, 1)

            def hidden(i, u):
                act.wait_ge(h_ps, i + 1)
                act.wait_ge(w1_done, i + 1)
                if not isinstance(i, int):
                    act.wait_ge(y_ps, i - 1)
                for c in range(FC):
                    nc.scalar.activation(hT[:, u, c, :], st_ps[:, u, c // 2, (c % 2) * TILE:(c % 2 + 1) * TILE],
                                         ACT.Gelu_apprx_tanh, bias=wbuf[:, u, O_B1 + c:O_B1 + c + 1]).then_inc(h_sb, 1)

            for u in range(2):
                hidden(u, u)
            with act.Fori(0, TILES // 2 - 1) as i:
                for u in range(2):
                    hidden(i * 2 + (u + 2), u)

        @block.vector
        def _(dve):
            def statistics(first, count, done):
                with dve.Fori(0, count // 4) as i:
                    for j in range(4):
                        nc.vector.bn_stats(stats[:, j, :], xs[:, i * 4 + (first + j), :]).then_inc(done, 1)
                    for j in range(4):
                        dve.wait_ge(done, i * 9 + (first // 4 * 9 + j + 1))
                        nc.vector.sem_inc(dve_passed)
                        nc.vector.bn_aggr(moments[:, j, :], stats[:, j, :]).then_inc(done, 1)
                    dve.wait_ge(done, i * 9 + (first // 4 * 9 + 8))
                    nc.vector.tensor_copy(mean[:, bass.ds(i * 4 + first, 4), :], moments[:, :, :]).then_inc(done, 1)
                    dve.wait_ge(done, i * 9 + (first // 4 * 9 + 9))

            for n in range(LOADS):
                dve.wait_ge(x_in[n], 16)
                statistics(n * XB, XB, mean_done)
            nc.vector.tensor_scalar(rstd[:, :], mean[:, :, 1], EPS, None, ALU.add).then_inc(mean_done, 1)

            with dve.Fori(0, B // CB // 2) as i:
                for u in range(2):
                    c = i * 2 + u
                    parts = vparts[:, bass.ds(c * CB, CB), :].rearrange("p b (h c) -> p (b h) c", c=VW)
                    v = st_ps[0:KV, u, 0, :].rearrange("p (h c) -> p h c", c=DK)
                    rest = v_rest[:, u, :].rearrange("p (h c) -> p h c", c=DK)
                    dve.wait_ge(v1_done, c + 1)
                    nc.vector.tensor_tensor(rest, v, parts[:, :, 0:DK], ALU.subtract).then_inc(v_chain, 1)
                    dve.wait_ge(v_chain, c * 3 + 1)
                    nc.vector.tensor_copy(parts[:, :, DK + 1:2 * DK + 1], rest).then_inc(v_chain, 1)
                    dve.wait_ge(v_chain, c * 3 + 2)
                    nc.vector.tensor_tensor(parts[:, :, 2 * DK + 2:3 * DK + 2], rest, parts[:, :, DK + 1:2 * DK + 1],
                                            ALU.subtract).then_inc(v_chain, 1)

            dve.wait_ge(rstd_done, 1)
            dve.wait_ge(weights_in, WEIGHT_LOADS)

            def step(k, u):
                def maxima(half):
                    dve.wait_ge(s_done, 2 * k - 1 + half)
                    if half == 0:
                        at(dve, st_done, 2 * k - 4)
                    nc.vector.tensor_reduce(
                        mx[:, 1 - u, half * HALF:(half + 1) * HALF].rearrange("p (a h) -> p a h", a=2),
                        s_ps[:, :, 0:GW].rearrange("p a (h k) -> p a h k", h=GH), AX.X, ALU.max).then_inc(max_done, 1)

                if has(k, 0):
                    at(dve, xnT_ps, k - 1)
                    nc.vector.tensor_scalar(xn[:, u, :], xs[:, k, :], mean[:, k, 0:1], rstd_of(k),
                                            ALU.subtract, ALU.mult).then_inc(xn_done, 1)
                if has(k, 0):
                    dve.wait_ge(kh_done, k + 1)
                    rows = kst[64:96, u]
                    nc.vector.tensor_tensor(rows, misc_ps[64:96, 0:NG * KV].rearrange("p (g k) -> p g k", g=NG),
                                            rows.bitcast(F32), ALU.subtract).then_inc(k_done, 1)
                if has(k, 1):
                    maxima(0)
                if has(k, 0):
                    dve.wait_ge(q_ps, k + 1)
                    at(dve, q_done, k)
                    nc.vector.tensor_tensor(qb[:, :, :], misc_ps[0:ROWS, :].rearrange("p (g t) -> p g t", g=NG),
                                            bq3[:, :].unsqueeze(2).broadcast_to([ROWS, NG, T]),
                                            ALU.add).then_inc(qb_done, 1)
                if has(k, 1):
                    maxima(1)
                if has(k, 3):
                    dve.wait_ge(av_done, k - 2)
                    at(dve, cc_done, k - 4)
                    nc.vector.tensor_reduce(osum[:, 1 - u], av_ps[:, 0:HEADS * VW].rearrange(
                        "p (h s c) -> p h c s", h=HEADS, s=3), AX.X, ALU.add).then_inc(osum_done, 1)
                if has(k, 0):
                    dve.wait_ge(qh_done, k + 1)
                    rows = qst[32:64, u]
                    nc.vector.tensor_tensor(rows, qb[32:64, :, :], rows.bitcast(F32), ALU.subtract).then_inc(q_done, 1)
                if has(k, 3):
                    dve.wait_ge(osum_done, k - 2)
                    nc.vector.reciprocal(rden[:, 1 - u, :], osum[:, 1 - u, :, DK]).then_inc(rden_done, 1)
                if has(k, 2):
                    for half in range(2):
                        dve.wait_ge(exp_done, 2 * k - 3 + half)
                        dve.wait_ge(p1_done, 2 * k - 3 + half)
                        hs = slice(half * HALF, (half + 1) * HALF)
                        if half == 0:
                            at(dve, av_done, k - 3)
                        nc.vector.tensor_tensor(p2[:, u, hs, :], p32[:, u, hs, :], p1[:, u, hs, :],
                                                ALU.subtract).then_inc(p2_done, 1)
                        if half == 0 and has(k, 3):
                            dve.wait_ge(rden_done, k - 2)
                            at(dve, ccT_ps, k - 4)
                            nc.vector.tensor_tensor(
                                cc[:, 1 - u, :].rearrange("p (h c) -> p h c", c=DK), osum[:, 1 - u, :, 0:DK],
                                rden[:, 1 - u, :].unsqueeze(2).broadcast_to([T, HEADS, DK]),
                                ALU.mult).then_inc(cc_done, 1)
                elif has(k, 3):
                    dve.wait_ge(rden_done, k - 2)
                    at(dve, ccT_ps, k - 4)
                    nc.vector.tensor_tensor(
                        cc[:, 1 - u, :].rearrange("p (h c) -> p h c", c=DK), osum[:, 1 - u, :, 0:DK],
                        rden[:, 1 - u, :].unsqueeze(2).broadcast_to([T, HEADS, DK]), ALU.mult).then_inc(cc_done, 1)
                if has(k, 4):
                    b = k - 4
                    dve.wait_ge(proj_done, k - 3)
                    dve.wait_ge(xbo_done, k - 3)
                    nc.vector.tensor_tensor(xs[:, b, :], misc_ps[:, 0:D], xs[:, b, :], ALU.add).then_inc(x2_done, 1)

            def rstd_of(k):
                return rstd[:, k:k + 1] if isinstance(k, int) else rstd[:, bass.ds(k, 1)]

            steps(dve, step)

            made = [0]

            def link(instruction):
                made[0] += 1
                instruction.then_inc(chain, 1)
                dve.wait_ge(chain, made[0])

            dve.wait_ge(x2_done, B)
            statistics(0, B, stat2)
            nc.vector.tensor_scalar(rstd[:, :], mean[:, :, 1], EPS, None, ALU.add).then_inc(stat2, 1)
            dve.wait_ge(rstd2, 1)

            def norm2(b, u, done):
                nc.vector.tensor_scalar(xn[:, u, :], xs[:, b, :], mean[:, b, 0:1], rstd[:, bass.ds(b, 1)],
                                        ALU.subtract, ALU.mult).then_inc(done, 1)

            for u in range(2):
                norm2(u, u, xn2_done)
            with dve.Fori(0, B // 2 - 1) as i:
                for u in range(2):
                    b = i * 2 + (u + 2)
                    dve.wait_ge(xn2T_ps, b - 1)
                    norm2(b, u, xn2_done)

            dve.wait_ge(gate_done, B)
            dve.wait_ge(wg_in, 32)
            link(nc.vector.tensor_tensor(logits[:, :, :], av_ps[:, 0:B * E].rearrange("p (b e) -> p b e", e=E),
                                         bg_rows[:, :].unsqueeze(1).broadcast_to([T, B, E]), ALU.add))
            link(nc.vector.tensor_reduce(row_stat[:, :], logits[:, :, :], AX.X, ALU.max))
            nc.vector.tensor_tensor(logits[:, :, :], logits[:, :, :],
                                    row_stat[:, :].unsqueeze(2).broadcast_to([T, B, E]),
                                    ALU.subtract).then_inc(logits_done, 1)
            dve.wait_ge(gate_exp, 1)
            link(nc.vector.tensor_reduce(row_stat[:, :], probs[:, :, :], AX.X, ALU.add))
            link(nc.vector.reciprocal(row_stat[:, :], row_stat[:, :]))
            link(nc.vector.tensor_tensor(probs[:, :, :], probs[:, :, :],
                                         row_stat[:, :].unsqueeze(2).broadcast_to([T, B, E]), ALU.mult))
            for c in range(2):
                pick = onehot[:, :, c, :]
                link(nc.vector.tensor_reduce(top[:, :, c], probs[:, :, :], AX.X, ALU.max))
                link(nc.vector.tensor_tensor(pick, probs[:, :, :], top[:, :, c].unsqueeze(2).broadcast_to([T, B, E]),
                                             ALU.is_equal))
                link(nc.vector.tensor_tensor(pick, pick, rank_e[:, :].unsqueeze(1).broadcast_to([T, B, E]), ALU.mult))
                link(nc.vector.tensor_reduce(row_stat[:, :], pick, AX.X, ALU.max))
                link(nc.vector.tensor_tensor(pick, pick, row_stat[:, :].unsqueeze(2).broadcast_to([T, B, E]),
                                             ALU.is_equal))
                if c == 0:
                    link(nc.vector.scalar_tensor_tensor(out=probs[:, :, :], in0=pick, scalar=-2.0, in1=probs[:, :, :],
                                                        op0=ALU.mult, op1=ALU.add))
            nc.vector.tensor_tensor(chosen[:, :, :], onehot[:, :, 0, :], onehot[:, :, 1, :],
                                    ALU.add).then_inc(chosen_done, 1)
            link(nc.vector.tensor_tensor(row_stat[:, :], top[:, :, 0], top[:, :, 1], ALU.add))
            link(nc.vector.tensor_scalar(row_stat[:, :], row_stat[:, :], 1e-8, None, ALU.add))
            link(nc.vector.reciprocal(row_stat[:, :], row_stat[:, :]))
            link(nc.vector.tensor_tensor(weight[:, :, :], top[:, :, 0:2],
                                         row_stat[:, :].unsqueeze(2).broadcast_to([T, B, 2]), ALU.mult))
            link(nc.vector.tensor_scalar(weight[:, :, :], weight[:, :, :], gate[:, 1:2], None, ALU.mult))
            dve.wait_ge(count_done, 2)
            link(nc.vector.tensor_copy(scan[:, 0], s_ps[:, 0, :].rearrange("p (b e) -> p b e", e=E)))
            a = 0
            step_ = 1
            while step_ < B:
                nc.vector.tensor_copy(scan[:, 1 - a, 0:step_, :], scan[:, a, 0:step_, :]).then_inc(chain, 1)
                made[0] += 1
                link(nc.vector.tensor_tensor(scan[:, 1 - a, step_:B, :], scan[:, a, step_:B, :],
                                             scan[:, a, 0:B - step_, :], ALU.add))
                a = 1 - a
                step_ *= 2
            total = scan[:, a, B - 1, :]
            link(nc.vector.tensor_scalar(ntile[:, :], total, float(TILE - 1), None, ALU.add))
            link(nc.vector.tensor_copy(ntile_i[:, :], ntile[:, :]))
            link(nc.vector.tensor_scalar(ntile_i[:, :], ntile_i[:, :], TILE.bit_length() - 1, None,
                                         ALU.arith_shift_right))
            link(nc.vector.tensor_copy(ntile[:, :], ntile_i[:, :]))
            link(nc.vector.tensor_copy(cum[:, 0, :], ntile[:, :]))
            c = 0
            step_ = 1
            while step_ < E:
                nc.vector.tensor_copy(cum[:, 1 - c, 0:step_], cum[:, c, 0:step_]).then_inc(chain, 1)
                made[0] += 1
                link(nc.vector.tensor_tensor(cum[:, 1 - c, step_:E], cum[:, c, step_:E], cum[:, c, 0:E - step_],
                                             ALU.add))
                c = 1 - c
                step_ *= 2
            link(nc.vector.tensor_tensor(first_row[:, :], cum[:, c, :], ntile[:, :], ALU.subtract))
            link(nc.vector.tensor_scalar(first_row[:, :], first_row[:, :], float(TILE), None, ALU.mult))
            link(nc.vector.tensor_tensor(place[:, :, :], scan[:, a], s_ps[:, 0, :].rearrange("p (b e) -> p b e", e=E),
                                         ALU.subtract))
            link(nc.vector.tensor_tensor(place[:, :, :], place[:, :, :],
                                         s_ps[:, 1, :].rearrange("p (b e) -> p b e", e=E), ALU.add))
            link(nc.vector.tensor_tensor(place[:, :, :], place[:, :, :],
                                         first_row[:, :].unsqueeze(1).broadcast_to([T, B, E]), ALU.add))
            link(nc.vector.tensor_tensor(onehot[:, :, :, :], onehot[:, :, :, :],
                                         place[:, :, :].unsqueeze(2).broadcast_to([T, B, 2, E]), ALU.mult))
            link(nc.vector.tensor_reduce(slot_f[:, :, :], onehot[:, :, :, :], AX.X, ALU.add))
            link(nc.vector.tensor_copy(slots[:, :, :], slot_f[:, :, :]))
            link(nc.vector.tensor_tensor(reached[:, :, :],
                                         tile_no[:, :].unsqueeze(2).broadcast_to([1, TILES, E - 1]),
                                         cum[0:1, c, 0:E - 1].unsqueeze(1).broadcast_to([1, TILES, E - 1]), ALU.is_ge))
            link(nc.vector.tensor_reduce(tile_f[:, :], reached[:, :, :], AX.X, ALU.add))
            nc.vector.tensor_copy(tile_expert[:, :], tile_f[:, :]).then_inc(table_done, 1)

            def dispatch(b, u):
                if not isinstance(b, int):
                    dve.wait_ge(scattered[u], (b - u) * 16)
                norm2(b, u, row_done)
                nc.vector.tensor_copy(slot_now[:, u, :], slots[:, b, :]).then_inc(row_done, 1)

            for u in range(2):
                dispatch(u, u)
            with dve.Fori(0, B // 2 - 1) as i:
                for u in range(2):
                    dispatch(i * 2 + (u + 2), u)

            dve.wait_ge(table_done, 1)
            dve.wait_ge(experts_in, 16 * (2 + 2 * FC))

            def tile_step(k, u):
                if has_tile(k, 0):
                    dve.wait_ge(xgT_ps, k + 1)
                    if has_tile(k, 2):
                        dve.wait_ge(h_ps, k - 1)
                    nc.vector.tensor_copy(xgT[:, u, :], misc_ps[:, 0:TILE]).then_inc(xgT_sb, 1)
                    idx = tile_expert[0:1, k:k + 1] if isinstance(k, int) else tile_expert[0:1, bass.ds(k, 1)]
                    e = dve.value_load(idx, min_val=0, max_val=E - 1)
                    if has_tile(k, 2):
                        dve.wait_ge(h_sb, (k - 1) * FC)
                    nc.vector.tensor_copy(wbuf[:, u, 0:O_W2], arena[:, bass.ds(e * BUNDLE, O_W2)]).then_inc(w1_done, 1)
                if has_tile(k, 2):
                    dve.wait_ge(y_ps, k - 1)
                    if has_tile(k, 4):
                        dve.wait_ge(y_out[u], (k - u) * 8 - 16)
                    nc.vector.tensor_tensor(yb[:, u], s_ps[:, u, 0:TILE].rearrange("p (s d) -> p s d", s=SUB),
                                            wbuf[:, u, O_B2:BUNDLE].unsqueeze(1).broadcast_to([128, SUB, D]), ALU.add).then_inc(y_done, 1)
                if has_tile(k, 0):
                    if has_tile(k, 2):
                        dve.wait_ge(y_done, k - 1)
                    nc.vector.tensor_copy(wbuf[:, u, O_W2:BUNDLE],
                                          arena[:, bass.ds(e * BUNDLE + O_W2, BUNDLE - O_W2)]).then_inc(w2_done, 1)

            tile_steps(dve, tile_step)

            def place_of(b, u):
                nc.vector.tensor_copy(slot_now[:, u, :], slots[:, b, :]).then_inc(slot_done, 1)

            def finish(b, u, later):
                dve.wait_ge(gathered[u], (b - u) * 16 + 32)
                if later:
                    dve.wait_ge(res_out[u], (b - u) * 8)
                nc.vector.scalar_tensor_tensor(out=result[:, u, :], in0=picked[:, u, 0, :],
                                               scalar=weight[:, b, 0:1], in1=xs[:, b, :],
                                               op0=ALU.mult, op1=ALU.add).then_inc(res_chain, 1)
                dve.wait_ge(res_chain, b + 1)
                nc.vector.scalar_tensor_tensor(out=result[:, u, :], in0=picked[:, u, 1, :],
                                               scalar=weight[:, b, 1:2], in1=result[:, u, :],
                                               op0=ALU.mult, op1=ALU.add).then_inc(res_done, 1)

            for u in range(2):
                dve.wait_ge(scattered[u], 16 * B)
            for u in range(2):
                place_of(u, u)
            for u in range(2):
                finish(u, u, False)
                place_of(u + 2, u)
            with dve.Fori(0, B // 2 - 2) as i:
                for u in range(2):
                    b = i * 2 + (u + 2)
                    finish(b, u, True)
                    place_of(b + 2, u)
            for u in range(2):
                finish(B - 2 + u, u, True)

        @block.tensor
        def _(pe):
            pe.wait_ge(const_made, ALL_CONSTS)
            pe.wait_ge(weights_in, WEIGHT_LOADS)
            pe.wait_ge(wo_scaled, 2)
            def values(c, u):
                first = isinstance(c, int)
                pe.wait_ge(ctx_in_u[u], 16 if first else (c - u) * 8 + 16)
                dst = misc_ps if u == 0 else av_ps
                for j in range(CB):
                    last = nc.tensor.transpose(dst[0:DC + 1, j * KV:(j + 1) * KV], ctx_rows[:, u, j, :],
                                               ident[0:KV, 0:KV])
                last.then_inc(ctxT_ps, 1)
                pe.wait_ge(ctxT_sb, c * 2 + 2)
                if not first:
                    pe.wait_ge(v_chain, c * 3 - 5)
                for j in range(CB):
                    last = nc.tensor.matmul(st_ps[0:KV, u, 0, j * D:(j + 1) * D],
                                            ctxT_now[:, u, j * KV:(j + 1) * KV], wv[:, :], start=True, stop=True)
                last.then_inc(v_ps, 1)

            for u in range(2):
                values(u, u)
            with pe.Fori(0, B // CB // 2 - 1) as i:
                for u in range(2):
                    values(i * 2 + (u + 2), u)

            def step(k, u):
                def scores_t(half):
                    if half == 0:
                        pe.wait_ge(max_done, 2 * k - 2)
                    at(pe, p1_done, 2 * k - 5 + half)
                    for n in range(HALF):
                        h = half * HALF + n
                        dst = st_ps[0:KV, half, n // GH, (n % GH) * T:(n % GH + 1) * T]
                        nc.tensor.matmul(dst, km[:, u, h // GH, h % GH, :], qst[:, u, h // GH, :],
                                         start=True, stop=False)
                        last = nc.tensor.matmul(dst, mx[:, u, h:h + 1].broadcast_to([T, KV]), neg_ident[:, :],
                                                start=False, stop=True)
                    last.then_inc(st_done, 1)

                def scores(half):
                    v = 1 - u
                    if half == 0:
                        pe.wait_ge(q_done, k)
                        pe.wait_ge(km_done, k)
                    at(pe, max_done, 2 * k - 2 + half)
                    for a in range(2):
                        g = half * 2 + a
                        last = nc.tensor.matmul(s_ps[:, a, 0:GW], qst[:, v, g, :],
                                                km[:, v, g].rearrange("p h k -> p (h k)"), start=True, stop=True)
                    last.then_inc(s_done, 1)

                if has(k, 2):
                    scores_t(0)
                    scores_t(1)
                if has(k, 0):
                    if has(k, LAST + 1):
                        pe.wait_ge(x2_done, k - 4)
                    else:
                        at(pe, qb_done, k)
                    for g in range(NG):
                        last = nc.tensor.matmul(misc_ps[0:ROWS, g * KV:(g + 1) * KV], wk3[:, g, :],
                                                ctxT[:, bass.ds(k * KV, KV)], start=True, stop=True)
                    last.then_inc(k_ps, 1)
                if has(k, 1):
                    scores(0)
                if has(k, 0):
                    pe.wait_ge(xn_done, k + 1)
                    pe.wait_ge(k_done, k + 1)
                    nc.tensor.transpose(misc_ps[:, 0:T], xn[:, u, :], ident[:, :]).then_inc(xnT_ps, 1)
                if has(k, 3):
                    v = 1 - u
                    b = k - 3
                    pe.wait_ge(p2_done, 2 * k - 4)
                    at(pe, osum_done, k - 3)
                    for h in range(HEADS):
                        nc.tensor.matmul(av_ps[:, h * VW:(h + 1) * VW], p1[:, v, h, :],
                                         vparts[:, b, h * VW:(h + 1) * VW], start=True, stop=False)
                        last = nc.tensor.matmul(av_ps[:, h * VW + DK + 1:(h + 1) * VW], p2[:, v, h, :],
                                                vparts[:, b, h * VW:h * VW + 2 * DK + 2], start=False, stop=True)
                    last.then_inc(av_done, 1)
                if has(k, 0):
                    pe.wait_ge(xnT_sb, k + 1)
                    for g in range(NG):
                        last = nc.tensor.matmul(misc_ps[0:ROWS, g * T:(g + 1) * T], wq3[:, g, :], xnT[:, u, :],
                                                start=True, stop=True)
                    last.then_inc(q_ps, 1)
                if has(k, 1):
                    scores(1)
                if has(k, 4):
                    pe.wait_ge(cc_done, k - 3)
                    if has(k, 0):
                        pe.wait_ge(qb_done, k + 1)
                    else:
                        at(pe, x2_done, k - 4)
                    nc.tensor.transpose(misc_ps[:, 0:T], cc[:, u, :], ident[:, :]).then_inc(ccT_ps, 1)
                    pe.wait_ge(ccT_sb, k - 3)
                    nc.tensor.matmul(misc_ps[:, 0:D], ccT[:, u, :], wo[:, :], start=True, stop=True).then_inc(proj_done, 1)

            pe.wait_ge(ctxT_sb, 2 * (B // CB))
            pe.wait_ge(v_chain, 3 * (B // CB) - 2)
            steps(pe, step)

            pe.wait_ge(osum_done, B)
            pe.wait_ge(x2_done, B)
            pe.wait_ge(wg_in, 32)
            with pe.Fori(0, B // 2) as i:
                for u in range(2):
                    b = i * 2 + u
                    pe.wait_ge(xn2_done, b + 1)
                    pe.wait_ge(xn2T_sb, b)
                    nc.tensor.transpose(misc_ps[:, 0:T], xn[:, u, :], ident[:, :]).then_inc(xn2T_ps, 1)
                    pe.wait_ge(xn2T_sb, b + 1)
                    nc.tensor.matmul(av_ps[:, bass.ds(b * E, E)], xnT[:, u, :], wg[:, :],
                                     start=True, stop=True).then_inc(gate_done, 1)
            pe.wait_ge(chosen_done, 1)
            pe.wait_ge(max_done, 2 * B)
            rows = chosen[:, :, :].rearrange("p b e -> p (b e)")
            nc.tensor.matmul(s_ps[:, 0, :], ones[:, :], rows, start=True, stop=True).then_inc(count_done, 1)
            nc.tensor.matmul(s_ps[:, 1, :], before[:, :], rows, start=True, stop=True).then_inc(count_done, 1)

            def tile_step(k, u):
                if has_tile(k, 0):
                    pe.wait_ge(xg_in[u], (k // 2) * 16 + 16 if isinstance(k, int) else (k - u) * 8 + 16)
                    at(pe, xgT_sb, k)
                    for s_ in range(SUB):
                        last = nc.tensor.transpose(misc_ps[:, s_ * 128:(s_ + 1) * 128], xg[:, u, s_, :], ident[:, :])
                    last.then_inc(xgT_ps, 1)
                if has_tile(k, 1):
                    v = 1 - u
                    pe.wait_ge(xgT_sb, k)
                    pe.wait_ge(w1_done, k)
                    if has_tile(k, 3):
                        pe.wait_ge(h_sb, (k - 2) * FC)
                    for c in range(FC):
                        last = nc.tensor.matmul(st_ps[:, v, c // 2, (c % 2) * TILE:(c % 2 + 1) * TILE],
                                                wbuf[:, v, c * 128:(c + 1) * 128], xgT[:, v, :], start=True, stop=True)
                    last.then_inc(h_ps, 1)
                if has_tile(k, 2):
                    pe.wait_ge(h_sb, (k - 1) * FC)
                    pe.wait_ge(w2_done, k - 1)
                    if has_tile(k, 4):
                        pe.wait_ge(y_done, k - 3)
                    for s_ in range(SUB):
                        for c in range(FC):
                            last = nc.tensor.matmul(s_ps[:, u, s_ * D:(s_ + 1) * D],
                                                    hT[:, u, c, s_ * 128:(s_ + 1) * 128],
                                                    wbuf[:, u, O_W2 + c * D:O_W2 + (c + 1) * D],
                                                    start=(c == 0), stop=(c == FC - 1))
                    last.then_inc(y_ps, 1)

            pe.wait_ge(table_done, 1)
            tile_steps(pe, tile_step)


_INS = ['x', 'ctx_512', 'g_xattn', 'g_ffn', 'L0_xattn_Wq', 'L0_xattn_bq', 'L0_xattn_Wk', 'L0_xattn_bk', 'L0_xattn_Wv',
        'L0_xattn_bv', 'L0_xattn_Wo', 'L0_xattn_bo', 'L0_ffn_Wg', 'L0_ffn_bg', 'L0_ffn_W1', 'L0_ffn_b1', 'L0_ffn_W2',
        'L0_ffn_b2']


def kernel(**inputs):
    import numpy as _np
    import concourse.bacc as _bacc
    from concourse import mybir as _mybir
    from concourse.bass_utils import run_bass_kernel_spmd as _run

    nc = _bacc.Bacc("TRN2", target_bir_lowering=False, num_devices=1)
    arrays, args = {}, []
    for name in _INS:
        a = _np.ascontiguousarray(inputs[name])
        arrays[f"in_{name}"] = a
        args.append(nc.dram_tensor(f"in_{name}", a.shape, _mybir.dt.from_np(a.dtype), kind="ExternalInput").ap())
    shape = inputs["x"].shape
    args.append(nc.dram_tensor("out_x", shape, _mybir.dt.float32, kind="ExternalOutput").ap())
    flamingo(nc, *args)
    return _run(nc, [arrays], core_ids=[0]).results[0]["out_x"]
```

```python
from contextlib import ExitStack

import concourse.bass as bass
from concourse import mybir

F32 = mybir.dt.float32
F32R = mybir.dt.float32r
F16 = mybir.dt.float16
BF16 = mybir.dt.bfloat16
I32 = mybir.dt.int32
ALU = mybir.AluOpType
ACT = mybir.ActivationFunctionType
AX = mybir.AxisListType

HEADS = 16
DK = 8
EPS = 1e-5
GH = 4
TERMS = 3
ROWS = TERMS * GH * DK
VW = 27


def at(eng, sem, value):
    if not isinstance(value, int) or value > 0:
        eng.wait_ge(sem, value)


def flamingo(nc, x, ctx_in, g_xattn, g_ffn, Wq, bq, Wk, bk, Wv, bv, Wo, bo, Wg, bg, W1, b1, W2, b2, out, STAGE=9):
    B, T, D = x.shape
    KV, DC = ctx_in.shape[1:]
    NG = HEADS // GH
    CB = 4
    LOADS = 8
    XB = B // LOADS
    GW = GH * KV
    HALF = HEADS // 2
    SCALE = float(1.0 / (DK ** 0.5))

    E, _, F = W1.shape
    FC = F // 128
    TILE = 256
    SUB = TILE // 128
    TILES = 2 * B * T // TILE + E
    O_B1 = F
    O_W2 = F + FC
    O_B2 = O_W2 + FC * D
    BUNDLE = O_B2 + D

    es = ExitStack()
    with es:
        routed = nc.dram_tensor("routed", (TILES * TILE, D), F32, kind="Internal").ap()
        expert_out = nc.dram_tensor("expert_out", (TILES * TILE, D), F32, kind="Internal").ap()

        def sb(name, shape, dt=F32):
            return es.enter_context(nc.sbuf_tensor(name, shape, dt))

        def ps(name, shape, dt=F32):
            return es.enter_context(nc.psum_tensor(name, shape, dt))

        def sem(name):
            return es.enter_context(nc.semaphore(name))

        ident = sb("ident", [128, 128])
        neg_ident = sb("neg_ident", [128, 128], F32R)
        headmask = sb("headmask", [ROWS, GH])
        wq3 = sb("wq3", [D, NG, ROWS])
        bq3 = sb("bq3", [ROWS, NG])
        wk3 = sb("wk3", [128, NG, ROWS])
        wv = sb("wv", [DC + 1, D])
        wo = sb("wo", [D, D])
        bo_rows = sb("bo_rows", [T, D])
        gate = sb("gate", [128, 2])
        xs = sb("xs", [T, B, D])
        mean = sb("mean", [T, B, 2])
        rstd = sb("rstd", [T, B])
        shift = sb("shift", [T, B])
        half_power = sb("half_power", [T, B])
        early_ctx = sb("early_ctx", [128, B * KV])
        ctxT = early_ctx[:, :]
        arena = sb("arena", [128, max(B * HEADS * VW // 2, E * BUNDLE)])
        vparts = arena[0:KV, 0:B * HEADS * VW // 2].bitcast(BF16).rearrange("p (b c) -> p b c", b=B)
        experts = arena[:, 0:E * BUNDLE].rearrange("p (e c) -> p e c", e=E)
        ctx_rows = sb("ctx_rows", [KV, 2, CB, DC + 1])
        ctxT_now = sb("ctxT_now", [DC + 1, 2, CB * KV])
        v_rest = sb("v_rest", [KV, 2, CB * D])
        stats = sb("stats", [T, 4, 6])
        moments = sb("moments", [T, 4, 2])
        xn = sb("xn", [T, 2, D])
        xnT = sb("xnT", [D, 2, T])
        kst = sb("kst", [ROWS, 2, NG, KV], F32R)
        km = sb("km", [128, 2, NG, GH, KV], F32R)
        qb = sb("qb", [ROWS, NG, T])
        qst = sb("qst", [128, 2, NG, T], F32R)
        mx = sb("mx", [T, 2, HEADS], F32R)
        early_p = sb("early_p", [128, 2 * HEADS * T])
        p32 = early_p[0:KV, :].rearrange("p (u h q) -> p u h q", u=2, q=T)
        p1 = sb("p1", [KV, 2, HEADS, T], F16)
        p2 = sb("p2", [KV, 2, HEADS, T], F16)
        osum = sb("osum", [T, 2, HEADS, DK + 1])
        rden = sb("rden", [T, 2, HEADS])
        cc = sb("cc", [T, 2, D])
        ccT = sb("ccT", [D, 2, T])

        wg = sb("wg", [D, E])
        bg_rows = sb("bg_rows", [T, E])
        rank_e = sb("rank_e", [T, E])
        ones = sb("ones", [T, T], BF16)
        before = sb("before", [T, T], BF16)
        logits = sb("logits", [T, B, E])
        probs = sb("probs", [T, B, E])
        row_stat = sb("row_stat", [T, B])
        top = sb("top", [T, B, 2])
        onehot = sb("onehot", [T, B, 2, E])
        chosen = sb("chosen", [T, B, E], BF16)
        weight = sb("weight", [T, B, 2])
        scan = sb("scan", [T, 2, B, E])
        place = sb("place", [T, B, E])
        slot_f = sb("slot_f", [T, B, 2])
        slots = sb("slots", [T, B, 2], I32)
        ntile = sb("ntile", [T, E])
        ntile_i = sb("ntile_i", [T, E], I32)
        cum = sb("cum", [T, 2, E])
        first_row = sb("first_row", [T, E])
        tile_no = sb("tile_no", [1, TILES])
        reached = sb("reached", [1, TILES, E - 1])
        tile_f = sb("tile_f", [1, TILES])
        tile_expert = sb("tile_expert", [1, TILES], I32)
        zeros = sb("zeros", [128, SUB * D])
        slot_now = sb("slot_now", [T, 2, 2], I32)

        def part(space, start, *dims):
            size = 1
            for d in dims:
                size *= d
            view = space[:, start:start + size]
            if len(dims) == 2:
                return view.rearrange("p (a b) -> p a b", b=dims[1])
            return view.rearrange("p (a b c) -> p a b c", b=dims[1], c=dims[2])

        wbuf = part(early_ctx, 0, 2, BUNDLE)
        hT = part(early_ctx, 2 * BUNDLE, 2, FC, TILE)
        xg = part(early_p, 0, 2, SUB, D)
        xgT = part(early_p, 2 * TILE, 2, TILE)
        yb = part(early_p, 4 * TILE, 2, SUB, D)
        picked = part(early_p, 6 * TILE, 2, 2, D)
        result = part(early_p, 8 * TILE, 2, D)

        s_ps = ps("s_ps", [T, 2, 512])
        st_ps = ps("st_ps", [128, 2, 2, 512])
        av_ps = ps("av_ps", [T, 512])
        misc_ps = ps("misc_ps", [128, 512])

        const_made = sem("const_made")
        weights_in = sem("weights_in")
        x_in = [sem(f"x_in{i}") for i in range(LOADS)]
        ctx_in_u = [sem(f"ctx_in{u}") for u in range(2)]
        gates_done = sem("gates_done")
        wo_scaled = sem("wo_scaled")
        bo_scaled = sem("bo_scaled")
        mean_done = sem("mean_done")
        rstd_done = sem("rstd_done")
        ctxT_ps = sem("ctxT_ps")
        ctxT_sb = sem("ctxT_sb")
        v_ps = sem("v_ps")
        v1_done = sem("v1_done")
        v_chain = sem("v_chain")
        xn_done = sem("xn_done")
        xnT_ps = sem("xnT_ps")
        xnT_sb = sem("xnT_sb")
        k_ps = sem("k_ps")
        kh_done = sem("kh_done")
        k_done = sem("k_done")
        km_done = sem("km_done")
        q_ps = sem("q_ps")
        qb_done = sem("qb_done")
        qh_done = sem("qh_done")
        q_done = sem("q_done")
        s_done = sem("s_done")
        max_done = sem("max_done")
        st_done = sem("st_done")
        exp_done = sem("exp_done")
        p1_done = sem("p1_done")
        p2_done = sem("p2_done")
        av_done = sem("av_done")
        osum_done = sem("osum_done")
        rden_done = sem("rden_done")
        cc_done = sem("cc_done")
        ccT_ps = sem("ccT_ps")
        ccT_sb = sem("ccT_sb")
        proj_done = sem("proj_done")
        x2_done = sem("x2_done")
        xbo_done = sem("xbo_done")
        stored = sem("stored")
        chain = sem("chain")
        pool_passed = sem("pool_passed")
        dve_passed = sem("dve_passed")
        zeros_made = sem("zeros_made")
        wg_in = sem("wg_in")
        experts_in = sem("experts_in")
        stat2 = sem("stat2")
        rstd2 = sem("rstd2")
        xn2_done = sem("xn2_done")
        xn2T_ps = sem("xn2T_ps")
        xn2T_sb = sem("xn2T_sb")
        gate_done = sem("gate_done")
        logits_done = sem("logits_done")
        gate_exp = sem("gate_exp")
        chosen_done = sem("chosen_done")
        count_done = sem("count_done")
        table_done = sem("table_done")
        row_done = sem("row_done")
        scattered = [sem(f"scattered{u}") for u in range(2)]
        cleared = sem("cleared")
        xg_in = [sem(f"xg_in{u}") for u in range(2)]
        w1_done = sem("w1_done")
        w2_done = sem("w2_done")
        xgT_ps = sem("xgT_ps")
        xgT_sb = sem("xgT_sb")
        h_ps = sem("h_ps")
        h_sb = sem("h_sb")
        y_ps = sem("y_ps")
        y_done = sem("y_done")
        y_out = [sem(f"y_out{u}") for u in range(2)]
        slot_done = sem("slot_done")
        gathered = [sem(f"gathered{u}") for u in range(2)]
        res_chain = sem("res_chain")
        res_done = sem("res_done")
        res_out = [sem(f"res_out{u}") for u in range(2)]

        block = es.enter_context(nc.Block())
        STATS_DONE = B // 4 * 9
        KEYS_CLEAR = 6 + 2 * TERMS
        ALL_CONSTS = 13 + 2 * TERMS + 3
        LAST = 6

        def steps(eng, step):
            for k in range(LAST):
                step(k, k % 2)
            with eng.Fori(0, (B - LAST) // 2) as i:
                for u in range(2):
                    step(i * 2 + (LAST + u), u)
            for k in range(B, B + LAST):
                step(k, k % 2)

        def tile_steps(eng, step):
            for k in range(4):
                step(k, k % 2)
            with eng.Fori(0, (TILES - 4) // 2) as i:
                for u in range(2):
                    step(i * 2 + (4 + u), u)
            for k in range(TILES, TILES + 2):
                step(k, k % 2)

        def has_tile(k, lag):
            return not isinstance(k, int) or 0 <= k - lag < TILES

        def has(k, lag):
            return not isinstance(k, int) or 0 <= k - lag < B

        @block.sync
        def _(sp):
            def load_ctx(c, u):
                if isinstance(c, int):
                    at(sp, const_made, 3)
                else:
                    sp.wait_ge(ctxT_ps, c - 1)
                src = ctx_in[c * CB:(c + 1) * CB] if isinstance(c, int) else ctx_in[bass.ds(c * CB, CB)]
                sp.dma_start(ctx_rows[:, u, :, 0:DC], src.rearrange("b p d -> p b d")).then_inc(ctx_in_u[u], 16)

            for t in range(TERMS):
                sp.dma_start(wq3[:, :, 32 * t:32 * t + 32],
                             Wq.rearrange("d (g i) -> d g i", g=NG)).then_inc(weights_in, 16)
                sp.dma_start(wk3[0:DC, :, 32 * t:32 * t + 32],
                             Wk.rearrange("d (g i) -> d g i", g=NG)).then_inc(weights_in, 16)
                with nc.allow_non_contiguous_dma("one bias row per partition"):
                    sp.dma_start(bq3[32 * t:32 * t + 32, :],
                                 bq.rearrange("(g i) -> i g", g=NG)).then_inc(weights_in, 16)
            sp.dma_start(wv[0:DC, :], Wv).then_inc(weights_in, 16)
            sp.dma_start(wv[DC:DC + 1, :], bv.rearrange("(a n) -> a n", a=1)).then_inc(weights_in, 16)
            for u in range(2):
                load_ctx(u, u)
            sp.wait_ge(const_made, KEYS_CLEAR)
            for t in range(TERMS):
                sp.dma_start(wk3[DC:DC + 1, :, 32 * t:32 * t + 32],
                             bk.rearrange("(a g i) -> a g i", a=1, g=NG)).then_inc(weights_in, 16)
            for n in range(LOADS):
                sp.dma_start(xs[:, n * XB:(n + 1) * XB, :],
                             x[n * XB:(n + 1) * XB].rearrange("b p d -> p b d")).then_inc(x_in[n], 16)
            with sp.Fori(0, B // CB // 2 - 1) as i:
                for u in range(2):
                    load_ctx(i * 2 + (u + 2), u)
            sp.wait_ge(zeros_made, 1)
            sp.dma_start(routed.rearrange("(i p s) d -> p i (s d)", p=128, s=SUB),
                         zeros[:, :].unsqueeze(1).broadcast_to([128, TILES, SUB * D])).then_inc(cleared, 16)
            if STAGE == 1:
                sp.wait_ge(x2_done, B)
                sp.dma_start(out.rearrange("b p d -> p b d"), xs[:, :, :]).then_inc(stored, 16)
                sp.wait_ge(stored, 16)

            sp.wait_ge(av_done, 2 * B)
            view = experts
            sp.dma_start(view[:, :, 0:F], W1.rearrange("e d f -> d e f")).then_inc(experts_in, 16)
            with nc.allow_non_contiguous_dma("one bias per partition"):
                for c in range(FC):
                    sp.dma_start(view[:, :, O_B1 + c], b1[:, c * 128:(c + 1) * 128].rearrange("e p -> p e")).then_inc(experts_in, 16)
            for c in range(FC):
                sp.dma_start(view[:, :, O_W2 + c * D:O_W2 + (c + 1) * D],
                             W2[:, c * 128:(c + 1) * 128, :].rearrange("e p d -> p e d")).then_inc(experts_in, 16)
            sp.dma_start(view[:, :, O_B2:BUNDLE], b2.partition_broadcast(128)).then_inc(experts_in, 16)
            for u in range(2):
                sp.wait_ge(scattered[u], 16 * B)

            def load_tile(i, u):
                if not isinstance(i, int):
                    sp.wait_ge(xgT_ps, i - 1)
                sp.dma_start(xg[:, u], routed[bass.ds(i * TILE, TILE), :].rearrange("(p s) d -> p s d", s=SUB)).then_inc(xg_in[u], 16)

            for u in range(2):
                load_tile(u, u)
            with sp.Fori(0, TILES // 2 - 1) as i:
                for u in range(2):
                    load_tile(i * 2 + (u + 2), u)

            with sp.Fori(0, B // 2) as i:
                for u in range(2):
                    b = i * 2 + u
                    sp.wait_ge(res_done, b + 1)
                    sp.dma_start(out[bass.ds(b, 1)].rearrange("a p d -> p (a d)"), result[:, u, :]).then_inc(res_out[u], 16)
            for u in range(2):
                sp.wait_ge(res_out[u], 16 * (B // 2))

        WEIGHT_LOADS = 16 * (4 * TERMS + 2)

        @block.gpsimd
        def _(pool):
            made = [0]

            def make(instruction):
                made[0] += 1
                instruction.then_inc(const_made, 1)
                pool.wait_ge(const_made, made[0])

            make(nc.gpsimd.memset(ident[:, :], 0.0))
            make(nc.gpsimd.affine_select(out=ident[:, :], in_=ident[:, :], compare_op=ALU.not_equal, fill=1.0,
                                         base=0, pattern=[[-1, 128]], channel_multiplier=1))
            make(nc.gpsimd.memset(ctx_rows[:, :, :, DC:DC + 1], 1.0))
            make(nc.gpsimd.memset(headmask[:, :], 1.0))
            for t in range(TERMS):
                rows = headmask[32 * t:32 * t + 32, :]
                make(nc.gpsimd.affine_select(out=rows, in_=rows, compare_op=ALU.is_ge, fill=0.0,
                                             base=0, pattern=[[-DK, GH]], channel_multiplier=1))
                make(nc.gpsimd.affine_select(out=rows, in_=rows, compare_op=ALU.is_ge, fill=0.0,
                                             base=DK - 1, pattern=[[DK, GH]], channel_multiplier=-1))
            make(nc.gpsimd.memset(ctxT[DC:128, :], 0.0))
            make(nc.gpsimd.memset(wk3[DC:128, :, :], 0.0))
            make(nc.gpsimd.memset(km[ROWS:128].bitcast(F32), 0.0))
            make(nc.gpsimd.memset(qst[ROWS:128].bitcast(F32), 0.0))
            make(nc.gpsimd.memset(half_power[:, :], -0.5))
            make(nc.gpsimd.memset(ones[:, :], 1.0))
            make(nc.gpsimd.affine_select(out=before[:, :], in_=ones[:, :], compare_op=ALU.is_gt, fill=0.0,
                                         base=0, pattern=[[1, T]], channel_multiplier=-1))
            make(nc.gpsimd.iota(rank_e[:, :], pattern=[[-1, E]], base=E, channel_multiplier=0,
                                allow_small_or_imprecise_dtypes=True))
            make(nc.gpsimd.iota(tile_no[:, :], pattern=[[1, TILES]], base=0, channel_multiplier=0,
                                allow_small_or_imprecise_dtypes=True))
            nc.gpsimd.memset(zeros[:, :], 0.0).then_inc(zeros_made, 1)
            vv = vparts.rearrange("p b (h c) -> p (b h) c", c=VW)
            make(nc.gpsimd.memset(vv[:, :, DK:DK + 1], 1.0))
            make(nc.gpsimd.memset(vv[:, :, 2 * DK + 1:2 * DK + 2], 0.0))
            make(nc.gpsimd.memset(vv[:, :, 3 * DK + 2:3 * DK + 3], 0.0))
            pool.wait_ge(mean_done, B // 4 * 9 + 1)
            nc.gpsimd.tensor_tensor(rstd[:, :], rstd[:, :], half_power[:, :], ALU.pow).then_inc(rstd_done, 1)

            def step(k, u):
                if has(k, 1):
                    b = k - 1
                    pool.wait_ge(xn_done, k)
                    pool.wait_ge(km_done, k)
                    if isinstance(k, int) and k == 1:
                        pool.wait_ge(bo_scaled, 1)
                    nc.gpsimd.tensor_tensor(xs[:, b, :], xs[:, b, :], bo_rows[:, :], ALU.add).then_inc(xbo_done, 1)
                    v = 1 - u
                    pool.wait_ge(qh_done, k)
                    pool.wait_ge(xbo_done, k)
                    rows = qst[32:64, v]
                    nc.gpsimd.tensor_tensor(rows, qb[32:64, :, :], rows.bitcast(F32), ALU.subtract).then_inc(q_done, 1)
                if has(k, 0):
                    pool.wait_ge(k_done, k + 1)
                    at(pool, q_done, k)
                    at(pool, st_done, 2 * k - 2)
                    nc.gpsimd.tensor_tensor(
                        km[0:ROWS, u], kst[:, u].bitcast(F32).unsqueeze(2).broadcast_to([ROWS, NG, GH, KV]),
                        headmask[:, :].unsqueeze(1).unsqueeze(3).broadcast_to([ROWS, NG, GH, KV]),
                        ALU.mult).then_inc(km_done, 1)

            steps(pool, step)

            pool.wait_ge(stat2, B // 4 * 9 + 1)
            nc.gpsimd.tensor_tensor(rstd[:, :], rstd[:, :], half_power[:, :], ALU.pow).then_inc(rstd2, 1)

            pool.wait_ge(cleared, 16)
            with pool.Fori(0, B // 2) as i:
                for u in range(2):
                    b = i * 2 + u
                    pool.wait_ge(row_done, b * 2 + 2)
                    nc.gpsimd.sem_inc(pool_passed)
                    for c in range(2):
                        nc.gpsimd.indirect_dma_start(
                            out=routed, out_offset=bass.IndirectOffsetOnAxis(ap=slot_now[:, u, c:c + 1], axis=0),
                            in_=xn[:, u, :], in_offset=None).then_inc(scattered[u], 16)

            def store_y(i, u):
                pool.wait_ge(y_done, i + 1)
                pool.dma_start(expert_out[bass.ds(i * TILE, TILE), :].rearrange("(p s) d -> p s d", s=SUB),
                               yb[:, u]).then_inc(y_out[u], 16)

            with pool.Fori(0, TILES // 2) as i:
                for u in range(2):
                    store_y(i * 2 + u, u)
            for u in range(2):
                pool.wait_ge(y_out[u], 16 * (TILES // 2))

            with pool.Fori(0, B // 2) as i:
                for u in range(2):
                    b = i * 2 + u
                    pool.wait_ge(slot_done, b + 1)
                    nc.gpsimd.sem_inc(pool_passed)
                    for c in range(2):
                        nc.gpsimd.indirect_dma_start(
                            out=picked[:, u, c, :], out_offset=None, in_=expert_out,
                            in_offset=bass.IndirectOffsetOnAxis(ap=slot_now[:, u, c:c + 1], axis=0)).then_inc(gathered[u], 16)

        @block.scalar
        def _(act):
            act.dma_start(wg[:, :], Wg).then_inc(wg_in, 16)
            act.dma_start(bg_rows[:, :], bg.partition_broadcast(T)).then_inc(wg_in, 16)
            act.dma_start(wo[:, :], Wo).then_inc(gates_done, 16)
            act.dma_start(bo_rows[:, :], bo.partition_broadcast(T)).then_inc(gates_done, 16)
            act.dma_start(gate[:, 0:1], g_xattn.partition_broadcast(128)).then_inc(gates_done, 16)
            act.dma_start(gate[:, 1:2], g_ffn.partition_broadcast(128)).then_inc(gates_done, 16)
            act.wait_ge(gates_done, 64)
            nc.scalar.activation(gate[:, :], gate[:, :], ACT.Tanh).then_inc(gates_done, 1)
            act.wait_ge(gates_done, 65)
            nc.scalar.activation(wo[:, :], wo[:, :], ACT.Copy, scale=gate[:, 0:1]).then_inc(wo_scaled, 1)
            nc.scalar.activation(bo_rows[:, :], bo_rows[:, :], ACT.Copy, scale=gate[:, 0:1]).then_inc(bo_scaled, 1)
            act.wait_ge(const_made, 2)
            nc.scalar.activation(neg_ident[:, :], ident[:, :], ACT.Copy, scale=-1.0).then_inc(wo_scaled, 1)

            with act.Fori(0, B // CB // 2) as i:
                for u in range(2):
                    c = i * 2 + u
                    act.wait_ge(ctxT_ps, c + 1)
                    src = misc_ps[0:DC + 1, 0:CB * KV] if u == 0 else av_ps[0:DC + 1, 0:CB * KV]
                    nc.scalar.activation(ctxT_now[:, u, :], src, ACT.Copy).then_inc(ctxT_sb, 1)
                    nc.scalar.activation(ctxT[0:DC + 1, bass.ds(c * (CB * KV), CB * KV)], src, ACT.Copy).then_inc(ctxT_sb, 1)
                    act.wait_ge(v_ps, c + 1)
                    nc.scalar.activation(
                        vparts[:, bass.ds(c * CB, CB), :].rearrange("p b (h c) -> p (b h) c", c=VW)[:, :, 0:DK],
                        st_ps[0:KV, u, 0, :].rearrange("p (h c) -> p h c", c=DK), ACT.Copy).then_inc(v1_done, 1)

            act.wait_ge(mean_done, STATS_DONE + 2)

            def step(k, u):
                def exp(half, dst, done):
                    nc.scalar.activation(dst[:, u, half * HALF:(half + 1) * HALF, :],
                                         st_ps[0:KV, half, :, :].rearrange("p a (h q) -> p (a h) q", q=T),
                                         ACT.Exp, scale=SCALE).then_inc(done, 1)

                if has(k, 5):
                    v = 1 - u
                    act.wait_ge(ccT_ps, k - 4)
                    at(act, proj_done, k - 5)
                    nc.scalar.activation(ccT[:, v, :], misc_ps[:, 0:T], ACT.Copy).then_inc(ccT_sb, 1)
                if has(k, 0):
                    at(act, xnT_ps, k - 1)
                    one = (lambda t: t[:, k:k + 1] if isinstance(k, int) else t[:, bass.ds(k, 1)])
                    nc.scalar.activation(xn[:, u, :], xs[:, k, :], ACT.Identity, bias=one(shift),
                                         scale=one(rstd)).then_inc(xn_done, 1)
                if has(k, 2):
                    act.wait_ge(st_done, 2 * k - 3)
                    at(act, p2_done, 4 * k - 12)
                    exp(0, p32, exp_done)
                if has(k, 0):
                    act.wait_ge(k_ps, k + 1)
                    at(act, km_done, k - 1)
                    nc.scalar.activation(kst[:, u], misc_ps[0:ROWS, 0:NG * KV].rearrange("p (g k) -> p g k", g=NG),
                                         ACT.Copy).then_inc(kh_done, 1)
                if has(k, 2):
                    at(act, av_done, 2 * k - 6)
                    exp(0, p1, p1_done)
                if has(k, 0):
                    act.wait_ge(xnT_ps, k + 1)
                    at(act, q_ps, k - 1)
                    nc.scalar.activation(xnT[:, u, :], misc_ps[:, 0:T], ACT.Copy).then_inc(xnT_sb, 1)
                if has(k, 2):
                    act.wait_ge(st_done, 2 * k - 2)
                    exp(1, p32, exp_done)
                    exp(1, p1, p1_done)
                if has(k, 0):
                    act.wait_ge(qb_done, k + 1)
                    at(act, st_done, 2 * k - 2)
                    nc.scalar.activation(qst[0:ROWS, u], qb[:, :, :], ACT.Copy).then_inc(qh_done, 1)

            steps(act, step)

            act.wait_ge(proj_done, B)
            with act.Fori(0, B // 2) as i:
                for u in range(2):
                    b = i * 2 + u
                    act.wait_ge(xn2T_ps, b + 1)
                    nc.scalar.activation(xnT[:, u, :], misc_ps[:, 0:T], ACT.Copy).then_inc(xn2T_sb, 1)
            act.wait_ge(logits_done, 1)
            nc.scalar.activation(probs[:, :, :], logits[:, :, :], ACT.Exp).then_inc(gate_exp, 1)

            def hidden(i, u):
                act.wait_ge(h_ps, i + 1)
                act.wait_ge(w1_done, i + 1)
                if not isinstance(i, int):
                    act.wait_ge(y_ps, i - 1)
                for c in range(FC):
                    nc.scalar.activation(hT[:, u, c, :], st_ps[:, u, c // 2, (c % 2) * TILE:(c % 2 + 1) * TILE],
                                         ACT.Gelu_apprx_tanh, bias=wbuf[:, u, O_B1 + c:O_B1 + c + 1]).then_inc(h_sb, 1)

            for u in range(2):
                hidden(u, u)
            with act.Fori(0, TILES // 2 - 1) as i:
                for u in range(2):
                    hidden(i * 2 + (u + 2), u)

        @block.vector
        def _(dve):
            def statistics(first, count, done):
                with dve.Fori(0, count // 4) as i:
                    for j in range(4):
                        nc.vector.bn_stats(stats[:, j, :], xs[:, i * 4 + (first + j), :]).then_inc(done, 1)
                    for j in range(4):
                        dve.wait_ge(done, i * 9 + (first // 4 * 9 + j + 1))
                        nc.vector.sem_inc(dve_passed)
                        nc.vector.bn_aggr(moments[:, j, :], stats[:, j, :]).then_inc(done, 1)
                    dve.wait_ge(done, i * 9 + (first // 4 * 9 + 8))
                    nc.vector.tensor_copy(mean[:, bass.ds(i * 4 + first, 4), :], moments[:, :, :]).then_inc(done, 1)
                    dve.wait_ge(done, i * 9 + (first // 4 * 9 + 9))

            for n in range(LOADS):
                dve.wait_ge(x_in[n], 16)
                statistics(n * XB, XB, mean_done)
            nc.vector.tensor_scalar(rstd[:, :], mean[:, :, 1], EPS, None, ALU.add).then_inc(mean_done, 1)

            with dve.Fori(0, B // CB // 2) as i:
                for u in range(2):
                    c = i * 2 + u
                    parts = vparts[:, bass.ds(c * CB, CB), :].rearrange("p b (h c) -> p (b h) c", c=VW)
                    v = st_ps[0:KV, u, 0, :].rearrange("p (h c) -> p h c", c=DK)
                    rest = v_rest[:, u, :].rearrange("p (h c) -> p h c", c=DK)
                    dve.wait_ge(v1_done, c + 1)
                    nc.vector.tensor_tensor(rest, v, parts[:, :, 0:DK], ALU.subtract).then_inc(v_chain, 1)
                    dve.wait_ge(v_chain, c * 3 + 1)
                    nc.vector.tensor_copy(parts[:, :, DK + 1:2 * DK + 1], rest).then_inc(v_chain, 1)
                    dve.wait_ge(v_chain, c * 3 + 2)
                    nc.vector.tensor_tensor(parts[:, :, 2 * DK + 2:3 * DK + 2], rest, parts[:, :, DK + 1:2 * DK + 1],
                                            ALU.subtract).then_inc(v_chain, 1)

            dve.wait_ge(rstd_done, 1)
            nc.vector.scalar_tensor_tensor(out=shift[:, :], in0=mean[:, :, 0], scalar=-1.0, in1=rstd[:, :],
                                           op0=ALU.mult, op1=ALU.mult).then_inc(mean_done, 1)
            dve.wait_ge(weights_in, WEIGHT_LOADS)

            def step(k, u):
                def maxima(g):
                    dve.wait_ge(s_done, 4 * k - 3 + g)
                    if g == 0:
                        at(dve, st_done, 2 * k - 4)
                    nc.vector.tensor_reduce(
                        mx[:, 1 - u, g * GH:(g + 1) * GH],
                        s_ps[:, g % 2, 0:GW].rearrange("p (h k) -> p h k", h=GH), AX.X, ALU.max).then_inc(max_done, 1)

                def low_part(g):
                    v = 1 - u
                    if g % 2 == 0:
                        dve.wait_ge(exp_done, 2 * k - 5 + g // 2)
                        dve.wait_ge(p1_done, 2 * k - 5 + g // 2)
                        at(dve, av_done, 2 * k - 9 + g // 2)
                    hs = slice(g * GH, (g + 1) * GH)
                    nc.vector.tensor_tensor(p2[:, v, hs, :], p32[:, v, hs, :], p1[:, v, hs, :],
                                            ALU.subtract).then_inc(p2_done, 1)

                if has(k, 3):
                    low_part(0)
                if has(k, 5):
                    b = k - 5
                    dve.wait_ge(proj_done, k - 4)
                    dve.wait_ge(xbo_done, k - 4)
                    nc.vector.tensor_tensor(xs[:, b, :], misc_ps[:, 0:D], xs[:, b, :], ALU.add).then_inc(x2_done, 1)
                if has(k, 3):
                    low_part(1)
                if has(k, 0):
                    dve.wait_ge(kh_done, k + 1)
                    rows = kst[64:96, u]
                    nc.vector.tensor_tensor(rows, misc_ps[64:96, 0:NG * KV].rearrange("p (g k) -> p g k", g=NG),
                                            rows.bitcast(F32), ALU.subtract).then_inc(k_done, 1)
                if has(k, 3):
                    low_part(2)
                if has(k, 4):
                    dve.wait_ge(av_done, 2 * k - 6)
                    at(dve, cc_done, k - 5)
                    nc.vector.tensor_reduce(osum[:, u], av_ps[:, 0:HEADS * VW].rearrange(
                        "p (h s c) -> p h c s", h=HEADS, s=3), AX.X, ALU.add).then_inc(osum_done, 1)
                if has(k, 3):
                    low_part(3)
                if has(k, 4):
                    dve.wait_ge(osum_done, k - 3)
                    nc.vector.reciprocal(rden[:, u, :], osum[:, u, :, DK]).then_inc(rden_done, 1)
                if has(k, 1):
                    maxima(0)
                if has(k, 4):
                    dve.wait_ge(rden_done, k - 3)
                    at(dve, ccT_ps, k - 5)
                    nc.vector.tensor_tensor(
                        cc[:, u, :].rearrange("p (h c) -> p h c", c=DK), osum[:, u, :, 0:DK],
                        rden[:, u, :].unsqueeze(2).broadcast_to([T, HEADS, DK]), ALU.mult).then_inc(cc_done, 1)
                if has(k, 1):
                    maxima(1)
                if has(k, 0):
                    dve.wait_ge(q_ps, k + 1)
                    at(dve, q_done, k)
                    nc.vector.tensor_tensor(qb[:, :, :], misc_ps[0:ROWS, :].rearrange("p (g t) -> p g t", g=NG),
                                            bq3[:, :].unsqueeze(2).broadcast_to([ROWS, NG, T]),
                                            ALU.add).then_inc(qb_done, 1)
                if has(k, 1):
                    maxima(2)
                    maxima(3)

            steps(dve, step)

            made = [0]

            def link(instruction):
                made[0] += 1
                instruction.then_inc(chain, 1)
                dve.wait_ge(chain, made[0])

            dve.wait_ge(x2_done, B)
            statistics(0, B, stat2)
            nc.vector.tensor_scalar(rstd[:, :], mean[:, :, 1], EPS, None, ALU.add).then_inc(stat2, 1)
            dve.wait_ge(rstd2, 1)

            def norm2(b, u, done):
                nc.vector.tensor_scalar(xn[:, u, :], xs[:, b, :], mean[:, b, 0:1], rstd[:, bass.ds(b, 1)],
                                        ALU.subtract, ALU.mult).then_inc(done, 1)

            for u in range(2):
                norm2(u, u, xn2_done)
            with dve.Fori(0, B // 2 - 1) as i:
                for u in range(2):
                    b = i * 2 + (u + 2)
                    dve.wait_ge(xn2T_ps, b - 1)
                    norm2(b, u, xn2_done)

            dve.wait_ge(gate_done, B)
            dve.wait_ge(wg_in, 32)
            link(nc.vector.tensor_tensor(logits[:, :, :], av_ps[:, 0:B * E].rearrange("p (b e) -> p b e", e=E),
                                         bg_rows[:, :].unsqueeze(1).broadcast_to([T, B, E]), ALU.add))
            link(nc.vector.tensor_reduce(row_stat[:, :], logits[:, :, :], AX.X, ALU.max))
            nc.vector.tensor_tensor(logits[:, :, :], logits[:, :, :],
                                    row_stat[:, :].unsqueeze(2).broadcast_to([T, B, E]),
                                    ALU.subtract).then_inc(logits_done, 1)
            dve.wait_ge(gate_exp, 1)
            link(nc.vector.tensor_reduce(row_stat[:, :], probs[:, :, :], AX.X, ALU.add))
            link(nc.vector.reciprocal(row_stat[:, :], row_stat[:, :]))
            link(nc.vector.tensor_tensor(probs[:, :, :], probs[:, :, :],
                                         row_stat[:, :].unsqueeze(2).broadcast_to([T, B, E]), ALU.mult))
            for c in range(2):
                pick = onehot[:, :, c, :]
                link(nc.vector.tensor_reduce(top[:, :, c], probs[:, :, :], AX.X, ALU.max))
                link(nc.vector.tensor_tensor(pick, probs[:, :, :], top[:, :, c].unsqueeze(2).broadcast_to([T, B, E]),
                                             ALU.is_equal))
                link(nc.vector.tensor_tensor(pick, pick, rank_e[:, :].unsqueeze(1).broadcast_to([T, B, E]), ALU.mult))
                link(nc.vector.tensor_reduce(row_stat[:, :], pick, AX.X, ALU.max))
                link(nc.vector.tensor_tensor(pick, pick, row_stat[:, :].unsqueeze(2).broadcast_to([T, B, E]),
                                             ALU.is_equal))
                if c == 0:
                    link(nc.vector.scalar_tensor_tensor(out=probs[:, :, :], in0=pick, scalar=-2.0, in1=probs[:, :, :],
                                                        op0=ALU.mult, op1=ALU.add))
            nc.vector.tensor_tensor(chosen[:, :, :], onehot[:, :, 0, :], onehot[:, :, 1, :],
                                    ALU.add).then_inc(chosen_done, 1)
            link(nc.vector.tensor_tensor(row_stat[:, :], top[:, :, 0], top[:, :, 1], ALU.add))
            link(nc.vector.tensor_scalar(row_stat[:, :], row_stat[:, :], 1e-8, None, ALU.add))
            link(nc.vector.reciprocal(row_stat[:, :], row_stat[:, :]))
            link(nc.vector.tensor_tensor(weight[:, :, :], top[:, :, 0:2],
                                         row_stat[:, :].unsqueeze(2).broadcast_to([T, B, 2]), ALU.mult))
            link(nc.vector.tensor_scalar(weight[:, :, :], weight[:, :, :], gate[:, 1:2], None, ALU.mult))
            dve.wait_ge(count_done, 2)
            link(nc.vector.tensor_copy(scan[:, 0], s_ps[:, 0, :].rearrange("p (b e) -> p b e", e=E)))
            a = 0
            step_ = 1
            while step_ < B:
                nc.vector.tensor_copy(scan[:, 1 - a, 0:step_, :], scan[:, a, 0:step_, :]).then_inc(chain, 1)
                made[0] += 1
                link(nc.vector.tensor_tensor(scan[:, 1 - a, step_:B, :], scan[:, a, step_:B, :],
                                             scan[:, a, 0:B - step_, :], ALU.add))
                a = 1 - a
                step_ *= 2
            total = scan[:, a, B - 1, :]
            link(nc.vector.tensor_scalar(ntile[:, :], total, float(TILE - 1), None, ALU.add))
            link(nc.vector.tensor_copy(ntile_i[:, :], ntile[:, :]))
            link(nc.vector.tensor_scalar(ntile_i[:, :], ntile_i[:, :], TILE.bit_length() - 1, None,
                                         ALU.arith_shift_right))
            link(nc.vector.tensor_copy(ntile[:, :], ntile_i[:, :]))
            link(nc.vector.tensor_copy(cum[:, 0, :], ntile[:, :]))
            c = 0
            step_ = 1
            while step_ < E:
                nc.vector.tensor_copy(cum[:, 1 - c, 0:step_], cum[:, c, 0:step_]).then_inc(chain, 1)
                made[0] += 1
                link(nc.vector.tensor_tensor(cum[:, 1 - c, step_:E], cum[:, c, step_:E], cum[:, c, 0:E - step_],
                                             ALU.add))
                c = 1 - c
                step_ *= 2
            link(nc.vector.tensor_tensor(first_row[:, :], cum[:, c, :], ntile[:, :], ALU.subtract))
            link(nc.vector.tensor_scalar(first_row[:, :], first_row[:, :], float(TILE), None, ALU.mult))
            link(nc.vector.tensor_tensor(place[:, :, :], scan[:, a], s_ps[:, 0, :].rearrange("p (b e) -> p b e", e=E),
                                         ALU.subtract))
            link(nc.vector.tensor_tensor(place[:, :, :], place[:, :, :],
                                         s_ps[:, 1, :].rearrange("p (b e) -> p b e", e=E), ALU.add))
            link(nc.vector.tensor_tensor(place[:, :, :], place[:, :, :],
                                         first_row[:, :].unsqueeze(1).broadcast_to([T, B, E]), ALU.add))
            link(nc.vector.tensor_tensor(onehot[:, :, :, :], onehot[:, :, :, :],
                                         place[:, :, :].unsqueeze(2).broadcast_to([T, B, 2, E]), ALU.mult))
            link(nc.vector.tensor_reduce(slot_f[:, :, :], onehot[:, :, :, :], AX.X, ALU.add))
            link(nc.vector.tensor_copy(slots[:, :, :], slot_f[:, :, :]))
            link(nc.vector.tensor_tensor(reached[:, :, :],
                                         tile_no[:, :].unsqueeze(2).broadcast_to([1, TILES, E - 1]),
                                         cum[0:1, c, 0:E - 1].unsqueeze(1).broadcast_to([1, TILES, E - 1]), ALU.is_ge))
            link(nc.vector.tensor_reduce(tile_f[:, :], reached[:, :, :], AX.X, ALU.add))
            nc.vector.tensor_copy(tile_expert[:, :], tile_f[:, :]).then_inc(table_done, 1)

            def dispatch(b, u):
                if not isinstance(b, int):
                    dve.wait_ge(scattered[u], (b - u) * 16)
                norm2(b, u, row_done)
                nc.vector.tensor_copy(slot_now[:, u, :], slots[:, b, :]).then_inc(row_done, 1)

            for u in range(2):
                dispatch(u, u)
            with dve.Fori(0, B // 2 - 1) as i:
                for u in range(2):
                    dispatch(i * 2 + (u + 2), u)

            dve.wait_ge(table_done, 1)
            dve.wait_ge(experts_in, 16 * (2 + 2 * FC))

            def tile_step(k, u):
                if has_tile(k, 0):
                    dve.wait_ge(xgT_ps, k + 1)
                    if has_tile(k, 2):
                        dve.wait_ge(h_ps, k - 1)
                    nc.vector.tensor_copy(xgT[:, u, :], misc_ps[:, 0:TILE]).then_inc(xgT_sb, 1)
                    idx = tile_expert[0:1, k:k + 1] if isinstance(k, int) else tile_expert[0:1, bass.ds(k, 1)]
                    e = dve.value_load(idx, min_val=0, max_val=E - 1)
                    if has_tile(k, 2):
                        dve.wait_ge(h_sb, (k - 1) * FC)
                    nc.vector.tensor_copy(wbuf[:, u, 0:O_W2], arena[:, bass.ds(e * BUNDLE, O_W2)]).then_inc(w1_done, 1)
                if has_tile(k, 2):
                    dve.wait_ge(y_ps, k - 1)
                    if has_tile(k, 4):
                        dve.wait_ge(y_out[u], (k - u) * 8 - 16)
                    nc.vector.tensor_tensor(yb[:, u], s_ps[:, u, 0:TILE].rearrange("p (s d) -> p s d", s=SUB),
                                            wbuf[:, u, O_B2:BUNDLE].unsqueeze(1).broadcast_to([128, SUB, D]), ALU.add).then_inc(y_done, 1)
                if has_tile(k, 0):
                    if has_tile(k, 2):
                        dve.wait_ge(y_done, k - 1)
                    nc.vector.tensor_copy(wbuf[:, u, O_W2:BUNDLE],
                                          arena[:, bass.ds(e * BUNDLE + O_W2, BUNDLE - O_W2)]).then_inc(w2_done, 1)

            tile_steps(dve, tile_step)

            def place_of(b, u):
                nc.vector.tensor_copy(slot_now[:, u, :], slots[:, b, :]).then_inc(slot_done, 1)

            def finish(b, u, later):
                dve.wait_ge(gathered[u], (b - u) * 16 + 32)
                if later:
                    dve.wait_ge(res_out[u], (b - u) * 8)
                nc.vector.scalar_tensor_tensor(out=result[:, u, :], in0=picked[:, u, 0, :],
                                               scalar=weight[:, b, 0:1], in1=xs[:, b, :],
                                               op0=ALU.mult, op1=ALU.add).then_inc(res_chain, 1)
                dve.wait_ge(res_chain, b + 1)
                nc.vector.scalar_tensor_tensor(out=result[:, u, :], in0=picked[:, u, 1, :],
                                               scalar=weight[:, b, 1:2], in1=result[:, u, :],
                                               op0=ALU.mult, op1=ALU.add).then_inc(res_done, 1)

            for u in range(2):
                dve.wait_ge(scattered[u], 16 * B)
            for u in range(2):
                place_of(u, u)
            for u in range(2):
                finish(u, u, False)
                place_of(u + 2, u)
            with dve.Fori(0, B // 2 - 2) as i:
                for u in range(2):
                    b = i * 2 + (u + 2)
                    finish(b, u, True)
                    place_of(b + 2, u)
            for u in range(2):
                finish(B - 2 + u, u, True)

        @block.tensor
        def _(pe):
            pe.wait_ge(const_made, ALL_CONSTS)
            pe.wait_ge(weights_in, WEIGHT_LOADS)
            pe.wait_ge(wo_scaled, 2)
            def values(c, u):
                first = isinstance(c, int)
                pe.wait_ge(ctx_in_u[u], 16 if first else (c - u) * 8 + 16)
                dst = misc_ps if u == 0 else av_ps
                for j in range(CB):
                    last = nc.tensor.transpose(dst[0:DC + 1, j * KV:(j + 1) * KV], ctx_rows[:, u, j, :],
                                               ident[0:KV, 0:KV])
                last.then_inc(ctxT_ps, 1)
                pe.wait_ge(ctxT_sb, c * 2 + 2)
                if not first:
                    pe.wait_ge(v_chain, c * 3 - 5)
                for j in range(CB):
                    last = nc.tensor.matmul(st_ps[0:KV, u, 0, j * D:(j + 1) * D],
                                            ctxT_now[:, u, j * KV:(j + 1) * KV], wv[:, :], start=True, stop=True)
                last.then_inc(v_ps, 1)

            for u in range(2):
                values(u, u)
            with pe.Fori(0, B // CB // 2 - 1) as i:
                for u in range(2):
                    values(i * 2 + (u + 2), u)

            def step(k, u):
                def scores_t(half):
                    if half == 0:
                        pe.wait_ge(max_done, 4 * k - 4)
                    at(pe, p1_done, 2 * k - 5 + half)
                    for n in range(HALF):
                        h = half * HALF + n
                        dst = st_ps[0:KV, half, n // GH, (n % GH) * T:(n % GH + 1) * T]
                        nc.tensor.matmul(dst, km[:, u, h // GH, h % GH, :], qst[:, u, h // GH, :],
                                         start=True, stop=False)
                        last = nc.tensor.matmul(dst, mx[:, u, h:h + 1].broadcast_to([T, KV]), neg_ident[:, :],
                                                start=False, stop=True)
                    last.then_inc(st_done, 1)

                def scores(g):
                    v = 1 - u
                    if g == 0:
                        pe.wait_ge(q_done, k)
                        pe.wait_ge(km_done, k)
                    at(pe, max_done, 4 * k - 5 + g)
                    nc.tensor.matmul(s_ps[:, g % 2, 0:GW], qst[:, v, g, :],
                                     km[:, v, g].rearrange("p h k -> p (h k)"),
                                     start=True, stop=True).then_inc(s_done, 1)

                def weighted(half):
                    b = k - 4
                    if half == 0:
                        pe.wait_ge(p2_done, 4 * k - 12)
                        at(pe, osum_done, k - 4)
                    for h in range(half * HALF, (half + 1) * HALF):
                        nc.tensor.matmul(av_ps[:, h * VW:(h + 1) * VW], p1[:, u, h, :],
                                         vparts[:, b, h * VW:(h + 1) * VW], start=True, stop=False)
                        last = nc.tensor.matmul(av_ps[:, h * VW + DK + 1:(h + 1) * VW], p2[:, u, h, :],
                                                vparts[:, b, h * VW:h * VW + 2 * DK + 2], start=False, stop=True)
                    last.then_inc(av_done, 1)

                if has(k, 5):
                    v = 1 - u
                    pe.wait_ge(cc_done, k - 4)
                    if has(k, 0) or isinstance(k, int) and k == B:
                        pe.wait_ge(qb_done, k)
                    else:
                        pe.wait_ge(x2_done, k - 5)
                    nc.tensor.transpose(misc_ps[:, 0:T], cc[:, v, :], ident[:, :]).then_inc(ccT_ps, 1)
                if has(k, 4):
                    weighted(0)
                if has(k, 5):
                    pe.wait_ge(ccT_sb, k - 4)
                    nc.tensor.matmul(misc_ps[:, 0:D], ccT[:, 1 - u, :], wo[:, :], start=True, stop=True).then_inc(proj_done, 1)
                if has(k, 2):
                    scores_t(0)
                if has(k, 0):
                    if has(k, 5):
                        pe.wait_ge(x2_done, k - 4)
                    else:
                        at(pe, qb_done, k)
                    for g in range(NG):
                        last = nc.tensor.matmul(misc_ps[0:ROWS, g * KV:(g + 1) * KV], wk3[:, g, :],
                                                ctxT[:, bass.ds(k * KV, KV)], start=True, stop=True)
                    last.then_inc(k_ps, 1)
                if has(k, 4):
                    weighted(1)
                if has(k, 2):
                    scores_t(1)
                if has(k, 0):
                    pe.wait_ge(xn_done, k + 1)
                    pe.wait_ge(k_done, k + 1)
                    nc.tensor.transpose(misc_ps[:, 0:T], xn[:, u, :], ident[:, :]).then_inc(xnT_ps, 1)
                if has(k, 1):
                    scores(0)
                    scores(1)
                if has(k, 0):
                    pe.wait_ge(xnT_sb, k + 1)
                    for g in range(NG):
                        last = nc.tensor.matmul(misc_ps[0:ROWS, g * T:(g + 1) * T], wq3[:, g, :], xnT[:, u, :],
                                                start=True, stop=True)
                    last.then_inc(q_ps, 1)
                if has(k, 1):
                    scores(2)
                    scores(3)

            pe.wait_ge(ctxT_sb, 2 * (B // CB))
            pe.wait_ge(v_chain, 3 * (B // CB) - 2)
            steps(pe, step)

            pe.wait_ge(osum_done, B)
            pe.wait_ge(x2_done, B)
            pe.wait_ge(wg_in, 32)
            with pe.Fori(0, B // 2) as i:
                for u in range(2):
                    b = i * 2 + u
                    pe.wait_ge(xn2_done, b + 1)
                    pe.wait_ge(xn2T_sb, b)
                    nc.tensor.transpose(misc_ps[:, 0:T], xn[:, u, :], ident[:, :]).then_inc(xn2T_ps, 1)
                    pe.wait_ge(xn2T_sb, b + 1)
                    nc.tensor.matmul(av_ps[:, bass.ds(b * E, E)], xnT[:, u, :], wg[:, :],
                                     start=True, stop=True).then_inc(gate_done, 1)
            pe.wait_ge(chosen_done, 1)
            pe.wait_ge(max_done, 4 * B)
            rows = chosen[:, :, :].rearrange("p b e -> p (b e)")
            nc.tensor.matmul(s_ps[:, 0, :], ones[:, :], rows, start=True, stop=True).then_inc(count_done, 1)
            nc.tensor.matmul(s_ps[:, 1, :], before[:, :], rows, start=True, stop=True).then_inc(count_done, 1)

            def tile_step(k, u):
                if has_tile(k, 0):
                    pe.wait_ge(xg_in[u], (k // 2) * 16 + 16 if isinstance(k, int) else (k - u) * 8 + 16)
                    at(pe, xgT_sb, k)
                    for s_ in range(SUB):
                        last = nc.tensor.transpose(misc_ps[:, s_ * 128:(s_ + 1) * 128], xg[:, u, s_, :], ident[:, :])
                    last.then_inc(xgT_ps, 1)
                if has_tile(k, 1):
                    v = 1 - u
                    pe.wait_ge(xgT_sb, k)
                    pe.wait_ge(w1_done, k)
                    if has_tile(k, 3):
                        pe.wait_ge(h_sb, (k - 2) * FC)
                    for c in range(FC):
                        last = nc.tensor.matmul(st_ps[:, v, c // 2, (c % 2) * TILE:(c % 2 + 1) * TILE],
                                                wbuf[:, v, c * 128:(c + 1) * 128], xgT[:, v, :], start=True, stop=True)
                    last.then_inc(h_ps, 1)
                if has_tile(k, 2):
                    pe.wait_ge(h_sb, (k - 1) * FC)
                    pe.wait_ge(w2_done, k - 1)
                    if has_tile(k, 4):
                        pe.wait_ge(y_done, k - 3)
                    for s_ in range(SUB):
                        for c in range(FC):
                            last = nc.tensor.matmul(s_ps[:, u, s_ * D:(s_ + 1) * D],
                                                    hT[:, u, c, s_ * 128:(s_ + 1) * 128],
                                                    wbuf[:, u, O_W2 + c * D:O_W2 + (c + 1) * D],
                                                    start=(c == 0), stop=(c == FC - 1))
                    last.then_inc(y_ps, 1)

            pe.wait_ge(table_done, 1)
            tile_steps(pe, tile_step)


_INS = ['x', 'ctx_512', 'g_xattn', 'g_ffn', 'L0_xattn_Wq', 'L0_xattn_bq', 'L0_xattn_Wk', 'L0_xattn_bk', 'L0_xattn_Wv',
        'L0_xattn_bv', 'L0_xattn_Wo', 'L0_xattn_bo', 'L0_ffn_Wg', 'L0_ffn_bg', 'L0_ffn_W1', 'L0_ffn_b1', 'L0_ffn_W2',
        'L0_ffn_b2']


def kernel(**inputs):
    import numpy as _np
    import concourse.bacc as _bacc
    from concourse import mybir as _mybir
    from concourse.bass_utils import run_bass_kernel_spmd as _run

    nc = _bacc.Bacc("TRN2", target_bir_lowering=False, num_devices=1)
    arrays, args = {}, []
    for name in _INS:
        a = _np.ascontiguousarray(inputs[name])
        arrays[f"in_{name}"] = a
        args.append(nc.dram_tensor(f"in_{name}", a.shape, _mybir.dt.from_np(a.dtype), kind="ExternalInput").ap())
    shape = inputs["x"].shape
    args.append(nc.dram_tensor("out_x", shape, _mybir.dt.float32, kind="ExternalOutput").ap())
    flamingo(nc, *args)
    return _run(nc, [arrays], core_ids=[0]).results[0]["out_x"]
```

```python
from contextlib import ExitStack

import concourse.bass as bass
from concourse import mybir

F32 = mybir.dt.float32
F32R = mybir.dt.float32r
F16 = mybir.dt.float16
BF16 = mybir.dt.bfloat16
I32 = mybir.dt.int32
ALU = mybir.AluOpType
ACT = mybir.ActivationFunctionType
AX = mybir.AxisListType

HEADS = 16
DK = 8
EPS = 1e-5
GH = 4
TERMS = 3
ROWS = TERMS * GH * DK
VW = 27


def at(eng, sem, value):
    if not isinstance(value, int) or value > 0:
        eng.wait_ge(sem, value)


def flamingo(nc, x, ctx_in, g_xattn, g_ffn, Wq, bq, Wk, bk, Wv, bv, Wo, bo, Wg, bg, W1, b1, W2, b2, out):
    B, T, D = x.shape
    KV, DC = ctx_in.shape[1:]
    NG = HEADS // GH
    CB = 4
    LOADS = 8
    XB = B // LOADS
    GW = GH * KV
    HALF = HEADS // 2
    SCALE = float(1.0 / (DK ** 0.5))

    E, _, F = W1.shape
    FC = F // 128
    TILE = 256
    SUB = TILE // 128
    TILES = 2 * B * T // TILE + E
    ROWS_DEEP = 4
    RB = 4
    PICKS = 4
    O_GATE = HEADS * VW
    O_B1 = F
    O_W2 = F + FC
    O_B2 = O_W2 + FC * D
    BUNDLE = O_B2 + D

    es = ExitStack()
    with es:
        routed = nc.dram_tensor("routed", (TILES * TILE, D + 1), F32, kind="Internal").ap()
        expert_out = nc.dram_tensor("expert_out", (2 * B * T + TILES * TILE, D), F32, kind="Internal").ap()

        def sb(name, shape, dt=F32):
            return es.enter_context(nc.sbuf_tensor(name, shape, dt))

        def ps(name, shape, dt=F32):
            return es.enter_context(nc.psum_tensor(name, shape, dt))

        def sem(name):
            return es.enter_context(nc.semaphore(name))

        ident = sb("ident", [128, 128])
        neg_ident = sb("neg_ident", [128, 128], F32R)
        headmask = sb("headmask", [ROWS, GH])
        wq3 = sb("wq3", [D, NG, ROWS])
        bq3 = sb("bq3", [ROWS, NG])
        wk3 = sb("wk3", [128, NG, ROWS])
        wv = sb("wv", [128, D])
        wo = sb("wo", [D, D])
        bo_rows = sb("bo_rows", [T, D])
        gate = sb("gate", [128, 2])
        xs = sb("xs", [T, B, D])
        mean = sb("mean", [T, B, 2])
        rstd = sb("rstd", [T, B])
        shift = sb("shift", [T, B])
        half_power = sb("half_power", [T, B])
        early_ctx = sb("early_ctx", [128, B * KV])
        ctxT = early_ctx[:, :]
        arena = sb("arena", [128, max(B * HEADS * VW // 2, E * (BUNDLE + F))])
        vparts = arena[0:KV, 0:B * HEADS * VW // 2].bitcast(BF16).rearrange("p (b c) -> p b c", b=B)
        experts = arena[:, 0:E * BUNDLE].rearrange("p (e c) -> p e c", e=E)
        w1_low = arena[:, E * BUNDLE:E * (BUNDLE + F)]
        ctx_rows = sb("ctx_rows", [KV, 2, CB, DC + 1])
        ctxT_now = sb("ctxT_now", [128, 2, CB * KV])
        v_rest = sb("v_rest", [KV, 2, CB * D])
        stats = sb("stats", [T, 6])
        moments = sb("moments", [T, 2, 2])
        xn = sb("xn", [T, 2, D])
        xnT = sb("xnT", [D, 2, T])
        xn2 = sb("xn2", [T, 2, D])
        v_now = sb("v_now", [KV, 2, HEADS * VW], BF16)
        xn2T = sb("xn2T", [D, 2, T])
        norm_consts = sb("norm_consts", [T, 2])
        norm2_tmp = sb("norm2_tmp", [T, 2])
        kst = sb("kst", [ROWS, 2, NG, KV], F32R)
        km = sb("km", [128, 2, NG, GH, KV], F32R)
        qb = sb("qb", [ROWS, NG, T])
        qst = sb("qst", [128, 2, NG, T], F32R)
        mx = sb("mx", [T, 2, HEADS], F32R)
        early_p = sb("early_p", [128, 2 * HEADS * T])
        p32 = early_p[0:KV, :].rearrange("p (u h q) -> p u h q", u=2, q=T)
        p1 = sb("p1", [KV, 2, HEADS, T], F16)
        p2 = sb("p2", [KV, 2, HEADS, T], F16)
        osum = sb("osum", [T, 2, HEADS, DK + 1])
        rden = sb("rden", [T, 2, HEADS])
        cc = sb("cc", [T, 2, D])
        ccT = sb("ccT", [D, 2, T])

        wg = sb("wg", [D, E])
        bg_rows = sb("bg_rows", [T, E])
        rank_e = sb("rank_e", [T, E])
        ones = sb("ones", [T, T], BF16)
        before = sb("before", [T, T], BF16)
        logits = sb("logits", [T, B, E])
        probs = sb("probs", [T, B, E])
        row_stat = sb("row_stat", [T, B])
        top = sb("top", [T, B, 2])
        onehot = sb("onehot", [T, B, 2, E])
        chosen = sb("chosen", [T, B, E], BF16)
        weight = sb("weight", [T, B, 2])
        scan = sb("scan", [T, 2, B, E])
        row_stats = scan[:, 0, :, 0:6]
        place = sb("place", [T, B, E])
        slot_f = sb("slot_f", [T, B, 2])
        slots = sb("slots", [T, B, 2], I32)
        ntile = sb("ntile", [T, E])
        ntile_i = sb("ntile_i", [T, E], I32)
        cum = sb("cum", [T, 2, E])
        first_row = sb("first_row", [T, E])
        tile_no = sb("tile_no", [1, TILES])
        reached = sb("reached", [1, TILES, E - 1])
        tile_f = sb("tile_f", [1, TILES])
        tile_expert = sb("tile_expert", [1, TILES], I32)
        zeros = sb("zeros", [128, SUB * (D + 1)])
        spare_row = sb("spare_row", [128, TILES, SUB], I32)
        result_row = sb("result_row", [T, B, 2], I32)
        row_first = sb("row_first", [128, 2, SUB], I32)
        row_now = sb("row_now", [128, 2, SUB], I32)
        slot_now = sb("slot_now", [T, ROWS_DEEP, 2], I32)

        def part(space, start, *dims):
            size = 1
            for d in dims:
                size *= d
            view = space[:, start:start + size]
            if len(dims) == 2:
                return view.rearrange("p (a b) -> p a b", b=dims[1])
            return view.rearrange("p (a b c) -> p a b c", b=dims[1], c=dims[2])

        wbuf = part(early_ctx, 0, 2, BUNDLE)
        hT = part(early_ctx, 2 * BUNDLE, 2, FC, TILE)
        nrow = part(early_ctx, 0, ROWS_DEEP, 2, D + 1)
        early_km = km[:, :, :, :, :].rearrange("p u g h k -> p (u g h k)")
        early_qst = qst[:, :, :, :].rearrange("p u g t -> p (u g t)")
        w1_now = part(early_km, 0, 2, F)
        w1_low_now = part(early_km, 2 * F, 2, F)
        xgT = part(early_qst, 0, 2, TILE)
        xgT_low = part(early_qst, 2 * TILE, 2, TILE)
        yb = part(early_p, 4 * TILE, 2, SUB, D)
        xg = part(early_p, 6 * TILE, 2, SUB, D + 1)
        picked = part(early_ctx, 0, PICKS, RB, 2 * D)

        pair_ps = ps("pair_ps", [T, 2, 512])
        s_ps = pair_ps[:, 0, :]
        small_ps = pair_ps[:, 1, :]
        st_ps = ps("st_ps", [128, 2, 2, 512])
        av_ps = ps("av_ps", [T, 512])
        misc_ps = ps("misc_ps", [128, 512])

        const_made = sem("const_made")
        weights_in = sem("weights_in")
        wv_in = sem("wv_in")
        v_in = [sem(f"v_in{u}") for u in range(2)]
        x_in = [sem(f"x_in{i}") for i in range(LOADS)]
        ctx_in_u = [sem(f"ctx_in{u}") for u in range(2)]
        gates_done = sem("gates_done")
        wo_scaled = sem("wo_scaled")
        bo_scaled = sem("bo_scaled")
        mean_done = sem("mean_done")
        rstd_done = sem("rstd_done")
        ctxT_ps = sem("ctxT_ps")
        ctxT_sb = sem("ctxT_sb")
        v_ps = sem("v_ps")
        v1_done = sem("v1_done")
        v_chain = sem("v_chain")
        xn_done = sem("xn_done")
        xnT_ps = sem("xnT_ps")
        xnT_sb = sem("xnT_sb")
        k_ps = sem("k_ps")
        kh_done = sem("kh_done")
        k_done = sem("k_done")
        km_done = sem("km_done")
        q_ps = sem("q_ps")
        qb_done = sem("qb_done")
        qh_done = sem("qh_done")
        q_done = sem("q_done")
        s_done = sem("s_done")
        max_done = sem("max_done")
        st_done = sem("st_done")
        exp_done = sem("exp_done")
        p1_done = sem("p1_done")
        p2_done = sem("p2_done")
        av_done = sem("av_done")
        osum_done = sem("osum_done")
        rden_done = sem("rden_done")
        cc_done = sem("cc_done")
        ccT_ps = sem("ccT_ps")
        ccT_sb = sem("ccT_sb")
        proj_done = sem("proj_done")
        x2_done = sem("x2_done")
        xbo_done = sem("xbo_done")
        stored = sem("stored")
        chain = sem("chain")
        pool_passed = sem("pool_passed")
        dve_passed = sem("dve_passed")
        wg_in = sem("wg_in")
        experts_in = sem("experts_in")
        bn2_done = sem("bn2_done")
        stat2_done = sem("stat2_done")
        norm2_ready = sem("norm2_ready")
        xn2_done = sem("xn2_done")
        xn2T_ps = sem("xn2T_ps")
        xn2T_sb = sem("xn2T_sb")
        gate_done = sem("gate_done")
        logit_done = sem("logit_done")
        logits_done = sem("logits_done")
        gate_exp = sem("gate_exp")
        chosen_done = sem("chosen_done")
        count_done = sem("count_done")
        table_done = sem("table_done")
        row_done = sem("row_done")
        scattered = [sem(f"scattered{u}") for u in range(ROWS_DEEP)]
        cleared = sem("cleared")
        xg_in = [sem(f"xg_in{u}") for u in range(2)]
        w1_split = sem("w1_split")
        w1_done = sem("w1_done")
        w2_done = sem("w2_done")
        xgT_ps = sem("xgT_ps")
        xgT_high = sem("xgT_high")
        xgT_sb = sem("xgT_sb")
        h_ps = sem("h_ps")
        h_sb = sem("h_sb")
        y_ps = sem("y_ps")
        y_done = sem("y_done")
        y_out = [sem(f"y_out{u}") for u in range(2)]
        row_first_done = sem("row_first_done")
        row_now_done = sem("row_now_done")
        picked_in = [sem(f"picked_in{u}") for u in range(PICKS)]
        res_chain = sem("res_chain")
        res_done = sem("res_done")
        res_out = sem("res_out")

        block = es.enter_context(nc.Block())
        EARLY = B - XB
        STATS_DONE = B + 10
        VALUES_CLEAR = 6
        KEYS_CLEAR = 8 + 2 * TERMS
        ALL_CONSTS = 20 + 2 * TERMS + 3
        LAST = 10

        def steps(eng, step):
            for k in range(LAST):
                step(k, k % 2)
            with eng.Fori(0, (B - LAST) // 2) as i:
                for u in range(2):
                    step(i * 2 + (LAST + u), u)
            for k in range(B, B + LAST):
                step(k, k % 2)

        def tile_steps(eng, step):
            for k in range(4):
                step(k, k % 2)
            with eng.Fori(0, (TILES - 4) // 2) as i:
                for u in range(2):
                    step(i * 2 + (4 + u), u)
            for k in range(TILES, TILES + 2):
                step(k, k % 2)

        def has_tile(k, lag):
            return not isinstance(k, int) or 0 <= k - lag < TILES

        def has(k, lag):
            return not isinstance(k, int) or 0 <= k - lag < B

        MISC_USERS = ((0, k_done), (0, qb_done))
        KEYS, QUERIES = range(2)
        SMALL_USERS = ((5, ccT_sb), (5, x2_done), (0, xnT_sb), (7, xn2T_sb))
        CCT, PROJ, XNT, XN2T = range(4)

        def bank_free(pe, k, users, user):
            n = len(users)
            for back in range(1, n + 1):
                lag, read = users[(user - back) % n]
                step_ = k if back <= user else k - 1
                if has(step_, lag):
                    pe.wait_ge(read, step_ - lag + 1)
                    return

        @block.sync
        def _(sp):
            def load_ctx(c, u):
                if c < 2:
                    sp.wait_ge(const_made, 3)
                else:
                    sp.wait_ge(ctxT_ps, c - 1)
                src = ctx_in[c * CB:(c + 1) * CB]
                sp.dma_start(ctx_rows[:, u, :, 0:DC], src.rearrange("b p d -> p b d")).then_inc(ctx_in_u[u], 16)

            sp.dma_start(wv[0:DC, :], Wv).then_inc(wv_in, 16)
            sp.wait_ge(const_made, VALUES_CLEAR)
            sp.dma_start(wv[DC:DC + 1, :], bv.rearrange("(a n) -> a n", a=1)).then_inc(wv_in, 16)
            for u in range(2):
                load_ctx(u, u)

            def load_x(n):
                sp.dma_start(xs[:, n * XB:(n + 1) * XB, :],
                             x[n * XB:(n + 1) * XB].rearrange("b p d -> p b d")).then_inc(x_in[n], 16)

            load_x(0)
            for t in range(TERMS):
                sp.dma_start(wq3[:, :, 32 * t:32 * t + 32],
                             Wq.rearrange("d (g i) -> d g i", g=NG)).then_inc(weights_in, 16)
                sp.dma_start(wk3[0:DC, :, 32 * t:32 * t + 32],
                             Wk.rearrange("d (g i) -> d g i", g=NG)).then_inc(weights_in, 16)
                with nc.allow_non_contiguous_dma("one bias row per partition"):
                    sp.dma_start(bq3[32 * t:32 * t + 32, :],
                                 bq.rearrange("(g i) -> i g", g=NG)).then_inc(weights_in, 16)
            for n in range(1, LOADS):
                for c in range(n * XB // CB, (n + 1) * XB // CB):
                    load_ctx(c, c % 2)
                load_x(n)
            sp.wait_ge(const_made, KEYS_CLEAR)
            for t in range(TERMS):
                sp.dma_start(wk3[DC:DC + 1, :, 32 * t:32 * t + 32],
                             bk.rearrange("(a g i) -> a g i", a=1, g=NG)).then_inc(weights_in, 16)
            sp.wait_ge(const_made, ALL_CONSTS)
            sp.dma_start(routed.rearrange("(i p s) d -> p i (s d)", p=128, s=SUB),
                         zeros[:, :].unsqueeze(1).broadcast_to([128, TILES, SUB * (D + 1)])).then_inc(cleared, 16)
            sp.wait_ge(cleared, 16)
            with nc.allow_non_contiguous_dma("one number per row"):
                for s_ in range(SUB):
                    sp.dma_start(routed.rearrange("(i p s) d -> p i s d", p=128, s=SUB)[:, :, s_, D],
                                 spare_row[:, :, s_].bitcast(F32)).then_inc(cleared, 16)
            def load_values(b, u):
                if not isinstance(b, int):
                    sp.wait_ge(av_done, 2 * b - 2)
                sp.dma_start(v_now[:, u, :], vparts[:, bass.ds(b, 1), :].rearrange("p a c -> p (a c)")).then_inc(v_in[u], 16)

            sp.wait_ge(v_chain, 3 * (B // CB))
            for u in range(2):
                load_values(u, u)
            with sp.Fori(0, B // 2 - 1) as i:
                for u in range(2):
                    load_values(i * 2 + (u + 2), u)

            sp.wait_ge(av_done, 2 * B)
            view = experts
            sp.dma_start(view[:, :, 0:F], W1.rearrange("e d f -> d e f")).then_inc(experts_in, 16)
            sp.dma_start(w1_low.rearrange("p (e f) -> p e f", e=E), W1.rearrange("e d f -> d e f")).then_inc(experts_in, 16)
            with nc.allow_non_contiguous_dma("one bias per partition"):
                for c in range(FC):
                    sp.dma_start(view[:, :, O_B1 + c], b1[:, c * 128:(c + 1) * 128].rearrange("e p -> p e")).then_inc(experts_in, 16)
            for c in range(FC):
                sp.dma_start(view[:, :, O_W2 + c * D:O_W2 + (c + 1) * D],
                             W2[:, c * 128:(c + 1) * 128, :].rearrange("e p d -> p e d")).then_inc(experts_in, 16)
            sp.dma_start(view[:, :, O_B2:BUNDLE], b2.partition_broadcast(128)).then_inc(experts_in, 16)
            for u in range(ROWS_DEEP):
                sp.wait_ge(scattered[u], 32 * (B // ROWS_DEEP))

            def load_tile(i, u):
                if not isinstance(i, int):
                    sp.wait_ge(xgT_ps, i - 1)
                    sp.wait_ge(row_first_done, i - 1)
                sp.dma_start(xg[:, u], routed[bass.ds(i * TILE, TILE), :].rearrange("(p s) d -> p s d", s=SUB)).then_inc(xg_in[u], 16)

            for u in range(2):
                load_tile(u, u)
            with sp.Fori(0, TILES // 2 - 1) as i:
                for u in range(2):
                    load_tile(i * 2 + (u + 2), u)

            for u in range(2):
                sp.wait_ge(y_out[u], 16 * SUB * (TILES // 2))

            def load_picked(c, u):
                if not isinstance(c, int):
                    sp.wait_ge(res_done, (c - (PICKS - 1)) * RB)
                sp.dma_start(picked[:, u], expert_out[bass.ds(c * (RB * T * 2), RB * T * 2), :].rearrange(
                    "(b t c) d -> t b (c d)", b=RB, c=2)).then_inc(picked_in[u], 16)

            for u in range(PICKS):
                load_picked(u, u)
            with sp.Fori(0, B // RB // PICKS - 1) as i:
                for u in range(PICKS):
                    load_picked(i * PICKS + (u + PICKS), u)

        WEIGHT_LOADS = 16 * 4 * TERMS

        @block.gpsimd
        def _(pool):
            made = [0]

            def make(instruction):
                made[0] += 1
                instruction.then_inc(const_made, 1)
                pool.wait_ge(const_made, made[0])

            make(nc.gpsimd.memset(ident[:, :], 0.0))
            make(nc.gpsimd.affine_select(out=ident[:, :], in_=ident[:, :], compare_op=ALU.not_equal, fill=1.0,
                                         base=0, pattern=[[-1, 128]], channel_multiplier=1))
            make(nc.gpsimd.memset(ctx_rows[:, :, :, DC:DC + 1], 1.0))
            make(nc.gpsimd.memset(ctxT_now[DC:128], 0.0))
            make(nc.gpsimd.memset(wv[DC:128, :], 0.0))
            make(nc.gpsimd.memset(ctxT[DC:128, :], 0.0))
            make(nc.gpsimd.memset(headmask[:, :], 1.0))
            for t in range(TERMS):
                rows = headmask[32 * t:32 * t + 32, :]
                make(nc.gpsimd.affine_select(out=rows, in_=rows, compare_op=ALU.is_ge, fill=0.0,
                                             base=0, pattern=[[-DK, GH]], channel_multiplier=1))
                make(nc.gpsimd.affine_select(out=rows, in_=rows, compare_op=ALU.is_ge, fill=0.0,
                                             base=DK - 1, pattern=[[DK, GH]], channel_multiplier=-1))
            make(nc.gpsimd.memset(wk3[DC:128, :, :], 0.0))
            make(nc.gpsimd.memset(km[ROWS:128].bitcast(F32), 0.0))
            make(nc.gpsimd.memset(qst[ROWS:128].bitcast(F32), 0.0))
            make(nc.gpsimd.memset(half_power[:, :], -0.5))
            make(nc.gpsimd.memset(norm_consts[:, 0:1], EPS))
            make(nc.gpsimd.memset(norm_consts[:, 1:2], -1.0))
            make(nc.gpsimd.memset(ones[:, :], 1.0))
            make(nc.gpsimd.affine_select(out=before[:, :], in_=ones[:, :], compare_op=ALU.is_gt, fill=0.0,
                                         base=0, pattern=[[1, T]], channel_multiplier=-1))
            make(nc.gpsimd.iota(rank_e[:, :], pattern=[[-1, E]], base=E, channel_multiplier=0,
                                allow_small_or_imprecise_dtypes=True))
            make(nc.gpsimd.iota(tile_no[:, :], pattern=[[1, TILES]], base=0, channel_multiplier=0,
                                allow_small_or_imprecise_dtypes=True))
            make(nc.gpsimd.iota(result_row[:, :, :], pattern=[[2 * T, B], [1, 2]], base=0, channel_multiplier=2))
            make(nc.gpsimd.memset(zeros[:, :], 0.0))
            make(nc.gpsimd.iota(spare_row[:, :, :], pattern=[[TILE, TILES], [1, SUB]], base=2 * B * T,
                                channel_multiplier=SUB))
            vv = vparts.rearrange("p b (h c) -> p (b h) c", c=VW)
            make(nc.gpsimd.memset(vv[:, :, DK:DK + 1], 1.0))
            make(nc.gpsimd.memset(vv[:, :, 2 * DK + 1:2 * DK + 2], 0.0))
            make(nc.gpsimd.memset(vv[:, :, 3 * DK + 2:3 * DK + 3], 0.0))
            pool.wait_ge(mean_done, EARLY + 5)
            nc.gpsimd.tensor_tensor(rstd[:, 0:EARLY], rstd[:, 0:EARLY], half_power[:, 0:EARLY], ALU.pow).then_inc(rstd_done, 1)
            pool.wait_ge(mean_done, STATS_DONE)
            nc.gpsimd.tensor_tensor(rstd[:, EARLY:B], rstd[:, EARLY:B], half_power[:, EARLY:B], ALU.pow).then_inc(rstd_done, 1)

            def step(k, u):
                if has(k, 7):
                    b = k - 7
                    one = (lambda t: t[:, b:b + 1] if isinstance(b, int) else t[:, bass.ds(b, 1)])
                    pool.wait_ge(stat2_done, b + 1)
                    if has(k, 1):
                        pool.wait_ge(km_done, 2 * k)
                    nc.gpsimd.tensor_tensor(norm2_tmp[:, 0:1], moments[:, 1 - u, 1:2], norm_consts[:, 0:1],
                                            ALU.add).then_inc(norm2_ready, 1)
                    pool.wait_ge(norm2_ready, b * 4 + 1)
                    nc.gpsimd.sem_inc(pool_passed)
                    nc.gpsimd.tensor_tensor(one(rstd), norm2_tmp[:, 0:1], half_power[:, 0:1],
                                            ALU.pow).then_inc(norm2_ready, 1)
                    pool.wait_ge(norm2_ready, b * 4 + 2)
                    nc.gpsimd.sem_inc(pool_passed)
                    nc.gpsimd.tensor_tensor(norm2_tmp[:, 1:2], moments[:, 1 - u, 0:1], one(rstd),
                                            ALU.mult).then_inc(norm2_ready, 1)
                    pool.wait_ge(norm2_ready, b * 4 + 3)
                    nc.gpsimd.sem_inc(pool_passed)
                    nc.gpsimd.tensor_tensor(one(shift), norm2_tmp[:, 1:2], norm_consts[:, 1:2],
                                            ALU.mult).then_inc(norm2_ready, 1)
                if has(k, 1):
                    b = k - 1
                    pool.wait_ge(qh_done, b + 1)
                    if has(k, 7):
                        pool.wait_ge(norm2_ready, (k - 6) * 4)
                    else:
                        pool.wait_ge(km_done, 2 * b + 2)
                    rows = qst[32:64, 1 - u]
                    nc.gpsimd.tensor_tensor(rows, qb[32:64, :, :], rows.bitcast(F32), ALU.subtract).then_inc(q_done, 1)
                if has(k, 4):
                    b = k - 4
                    pool.wait_ge(xn_done, b + 1)
                    if has(k, 1):
                        pool.wait_ge(q_done, k)
                    if isinstance(b, int) and b == 0:
                        pool.wait_ge(bo_scaled, 1)
                    nc.gpsimd.tensor_tensor(xs[:, b, :], xs[:, b, :], bo_rows[:, :], ALU.add).then_inc(xbo_done, 1)
                if has(k, 0):
                    pool.wait_ge(k_done, k + 1)
                    if has(k, 4):
                        pool.wait_ge(xbo_done, k - 3)
                    elif has(k, 1):
                        pool.wait_ge(q_done, k)
                    for half in range(2):
                        at(pool, st_done, 2 * k - 3 + half)
                        gs = slice(half * NG // 2, (half + 1) * NG // 2)
                        nc.gpsimd.tensor_tensor(
                            km[0:ROWS, u, gs],
                            kst[:, u, gs].bitcast(F32).unsqueeze(2).broadcast_to([ROWS, NG // 2, GH, KV]),
                            headmask[:, :].unsqueeze(1).unsqueeze(3).broadcast_to([ROWS, NG // 2, GH, KV]),
                            ALU.mult).then_inc(km_done, 1)

            steps(pool, step)

            pool.wait_ge(cleared, 16 + 16 * SUB)
            with pool.Fori(0, B // ROWS_DEEP) as i:
                for u in range(ROWS_DEEP):
                    b = i * ROWS_DEEP + u
                    pool.wait_ge(row_done, b * 3 + 3)
                    nc.gpsimd.sem_inc(pool_passed)
                    for c in range(2):
                        nc.gpsimd.indirect_dma_start(
                            out=routed, out_offset=bass.IndirectOffsetOnAxis(ap=slot_now[:, u, c:c + 1], axis=0),
                            in_=nrow[:, u, c, :], in_offset=None).then_inc(scattered[u], 16)

            with pool.Fori(0, TILES // 2) as i:
                for u in range(2):
                    k = i * 2 + u
                    pool.wait_ge(row_now_done, k + 1)
                    pool.wait_ge(y_done, k + 1)
                    nc.gpsimd.sem_inc(pool_passed)
                    for s_ in range(SUB):
                        nc.gpsimd.indirect_dma_start(
                            out=expert_out, out_offset=bass.IndirectOffsetOnAxis(ap=row_now[:, u, s_:s_ + 1], axis=0),
                            in_=yb[:, u, s_, :], in_offset=None).then_inc(y_out[u], 16)

        @block.scalar
        def _(act):
            act.dma_start(wg[:, :], Wg).then_inc(wg_in, 16)
            act.dma_start(bg_rows[:, :], bg.partition_broadcast(T)).then_inc(wg_in, 16)
            act.dma_start(wo[:, :], Wo).then_inc(gates_done, 16)
            act.dma_start(bo_rows[:, :], bo.partition_broadcast(T)).then_inc(gates_done, 16)
            act.dma_start(gate[:, 0:1], g_xattn.partition_broadcast(128)).then_inc(gates_done, 16)
            act.dma_start(gate[:, 1:2], g_ffn.partition_broadcast(128)).then_inc(gates_done, 16)
            act.wait_ge(gates_done, 64)
            nc.scalar.activation(gate[:, :], gate[:, :], ACT.Tanh).then_inc(gates_done, 1)
            act.wait_ge(gates_done, 65)
            nc.scalar.activation(wo[:, :], wo[:, :], ACT.Copy, scale=gate[:, 0:1]).then_inc(wo_scaled, 1)
            nc.scalar.activation(bo_rows[:, :], bo_rows[:, :], ACT.Copy, scale=gate[:, 0:1]).then_inc(bo_scaled, 1)
            act.wait_ge(const_made, 2)
            nc.scalar.activation(neg_ident[:, :], ident[:, :], ACT.Copy, scale=-1.0).then_inc(wo_scaled, 1)

            def context(c, u):
                act.wait_ge(ctxT_ps, c + 1)
                if c >= 2 if isinstance(c, int) else True:
                    act.wait_ge(v_ps, c - 1)
                elif c == 0:
                    act.wait_ge(const_made, VALUES_CLEAR)
                src = misc_ps[0:DC + 1, 0:CB * KV] if u == 0 else av_ps[0:DC + 1, 0:CB * KV]
                nc.scalar.activation(ctxT_now[0:DC + 1, u, :], src, ACT.Copy).then_inc(ctxT_sb, 1)
                nc.scalar.activation(ctxT[0:DC + 1, bass.ds(c * (CB * KV), CB * KV)], src, ACT.Copy).then_inc(ctxT_sb, 1)

            def values_high(c, u):
                act.wait_ge(v_ps, c + 1)
                nc.scalar.activation(
                    vparts[:, bass.ds(c * CB, CB), :].rearrange("p b (h c) -> p (b h) c", c=VW)[:, :, 0:DK],
                    st_ps[0:KV, u, 0, :].rearrange("p (h c) -> p h c", c=DK), ACT.Copy).then_inc(v1_done, 1)

            for u in range(2):
                context(u, u)
            values_high(0, 0)
            with act.Fori(0, B // CB // 2 - 1) as i:
                for u in range(2):
                    c = i * 2 + (u + 2)
                    context(c, u)
                    values_high(c - 1, 1 - u)
            values_high(B // CB - 1, 1)

            act.wait_ge(mean_done, STATS_DONE + 1)

            def step(k, u):
                def high_part(b, v, half):
                    at(act, av_done, 2 * b - 3 + half)
                    exp(v, half, p1, p1_done)

                def exact(b, v, half):
                    at(act, p2_done, 4 * b - 6 + 2 * half)
                    act.wait_ge(st_done, 2 * b + 1 + half)
                    exp(v, half, p32, exp_done)

                def exp(v, half, dst, done):
                    nc.scalar.activation(dst[:, v, half * HALF:(half + 1) * HALF, :],
                                         st_ps[0:KV, half, :, :].rearrange("p a (h q) -> p (a h) q", q=T),
                                         ACT.Exp, scale=SCALE).then_inc(done, 1)

                def one(t, b):
                    return t[:, b:b + 1] if isinstance(b, int) else t[:, bass.ds(b, 1)]

                if has(k, 0):
                    nc.scalar.activation(xn[:, u, :], xs[:, k, :], ACT.Identity, bias=one(shift, k),
                                         scale=one(rstd, k)).then_inc(xn_done, 1)
                if has(k, 1):
                    b = k - 1
                    act.wait_ge(qb_done, b + 1)
                    nc.scalar.activation(qst[0:ROWS, 1 - u], qb[:, :, :], ACT.Copy).then_inc(qh_done, 1)
                if has(k, 3):
                    high_part(k - 3, 1 - u, 1)
                if has(k, 0):
                    act.wait_ge(k_ps, k + 1)
                    at(act, km_done, 2 * k - 2)
                    nc.scalar.activation(kst[:, u], misc_ps[0:ROWS, 0:NG * KV].rearrange("p (g k) -> p g k", g=NG),
                                         ACT.Copy).then_inc(kh_done, 1)
                    act.wait_ge(xnT_ps, k + 1)
                    nc.scalar.activation(xnT[:, u, :], small_ps[:, 0:T], ACT.Copy).then_inc(xnT_sb, 1)
                if has(k, 7):
                    b = k - 7
                    act.wait_ge(norm2_ready, 4 * b + 4)
                    nc.scalar.activation(xn2[:, 1 - u, :], xs[:, b, :], ACT.Identity, bias=one(shift, b),
                                         scale=one(rstd, b)).then_inc(xn2_done, 1)
                if has(k, 2):
                    exact(k - 2, u, 0)
                    exact(k - 2, u, 1)
                if has(k, 7):
                    b = k - 7
                    act.wait_ge(xn2T_ps, b + 1)
                    at(act, gate_done, b - 1)
                    nc.scalar.activation(xn2T[:, 1 - u, :], small_ps[:, 0:T], ACT.Copy).then_inc(xn2T_sb, 1)
                if has(k, 2):
                    high_part(k - 2, u, 0)
                if has(k, 4):
                    b = k - 4
                    act.wait_ge(ccT_ps, b + 1)
                    at(act, proj_done, b - 1)
                    nc.scalar.activation(ccT[:, u, :], small_ps[:, 0:T], ACT.Copy).then_inc(ccT_sb, 1)

            steps(act, step)

            act.wait_ge(logits_done, 1)
            nc.scalar.activation(probs[:, :, :], logits[:, :, :], ACT.Exp).then_inc(gate_exp, 1)

            act.wait_ge(experts_in, 16 * (3 + 2 * FC))
            nc.scalar.activation(experts[:, :, 0:F].bitcast(F32R), experts[:, :, 0:F], ACT.Copy).then_inc(w1_split, 1)

            def tile_step(k, u):
                if has_tile(k, 0):
                    act.wait_ge(xgT_ps, k + 1)
                    if has_tile(k, 2):
                        act.wait_ge(h_ps, k - 1)
                    nc.scalar.activation(xgT[:, u, :], misc_ps[:, 0:TILE], ACT.Copy).then_inc(xgT_high, 1)
                if has_tile(k, 1):
                    v = 1 - u
                    act.wait_ge(h_ps, k)
                    act.wait_ge(w2_done, k)
                    if has_tile(k, 3):
                        act.wait_ge(y_ps, k - 2)
                    for c in range(FC):
                        nc.scalar.activation(hT[:, v, c, :], st_ps[:, v, c // 2, (c % 2) * TILE:(c % 2 + 1) * TILE],
                                             ACT.Gelu_apprx_tanh, bias=wbuf[:, v, O_B1 + c:O_B1 + c + 1]).then_inc(h_sb, 1)

            tile_steps(act, tile_step)

            with act.Fori(0, B // RB) as i:
                act.wait_ge(res_done, i * RB + RB)
                act.dma_start(out[bass.ds(i * RB, RB)].rearrange("b p d -> p b d"),
                              xs[:, bass.ds(i * RB, RB), :]).then_inc(res_out, 16)
            act.wait_ge(res_out, 16 * (B // RB))

        @block.vector
        def _(dve):
            def value_parts(c, u):
                parts = vparts[:, c * CB:(c + 1) * CB, :].rearrange("p b (h c) -> p (b h) c", c=VW)
                v = st_ps[0:KV, u, 0, :].rearrange("p (h c) -> p h c", c=DK)
                rest = v_rest[:, u, :].rearrange("p (h c) -> p h c", c=DK)
                dve.wait_ge(v1_done, c + 1)
                nc.vector.tensor_tensor(rest, v, parts[:, :, 0:DK], ALU.subtract).then_inc(v_chain, 1)
                dve.wait_ge(v_chain, c * 3 + 1)
                nc.vector.tensor_copy(parts[:, :, DK + 1:2 * DK + 1], rest).then_inc(v_chain, 1)
                dve.wait_ge(v_chain, c * 3 + 2)
                nc.vector.tensor_tensor(parts[:, :, 2 * DK + 2:3 * DK + 2], rest, parts[:, :, DK + 1:2 * DK + 1],
                                        ALU.subtract).then_inc(v_chain, 1)

            def variances(first, last, ready):
                bs = slice(first, last)
                even, odd = row_stats[:, bs, 1:3], row_stats[:, bs, 4:6]
                dve.wait_ge(mean_done, ready)
                nc.vector.tensor_tensor(mean[:, bs, :], even, odd, ALU.add).then_inc(mean_done, 1)
                nc.vector.tensor_tensor(rstd[:, bs], even[:, :, 0], odd[:, :, 0], ALU.subtract).then_inc(mean_done, 1)
                dve.wait_ge(mean_done, ready + 2)
                nc.vector.tensor_tensor(rstd[:, bs], rstd[:, bs], rstd[:, bs], ALU.mult).then_inc(mean_done, 1)
                dve.wait_ge(mean_done, ready + 3)
                nc.vector.tensor_scalar(rstd[:, bs], rstd[:, bs], 0.25, EPS, ALU.mult, ALU.add).then_inc(mean_done, 1)
                dve.wait_ge(mean_done, ready + 4)
                nc.vector.scalar_tensor_tensor(out=rstd[:, bs], in0=mean[:, bs, 1], scalar=1.0 / D, in1=rstd[:, bs],
                                               op0=ALU.mult, op1=ALU.add).then_inc(mean_done, 1)

            for n in range(LOADS):
                dve.wait_ge(x_in[n], 16)
                for b in range(n * XB, (n + 1) * XB):
                    nc.vector.bn_stats(row_stats[:, b, :], xs[:, b, :]).then_inc(mean_done, 1)
                if n == LOADS - 2:
                    variances(0, EARLY, EARLY)
                elif n == LOADS - 1:
                    variances(EARLY, B, B + 5)
                for c in range(n * XB // CB, (n + 1) * XB // CB):
                    value_parts(c, c % 2)
            dve.wait_ge(rstd_done, 2)
            nc.vector.scalar_tensor_tensor(out=shift[:, :], in0=mean[:, :, 0], scalar=-0.5, in1=rstd[:, :],
                                           op0=ALU.mult, op1=ALU.mult).then_inc(mean_done, 1)
            dve.wait_ge(weights_in, WEIGHT_LOADS)

            def step(k, u):
                def low_part(g):
                    b = k - 3
                    v = 1 - u
                    half = g // 2
                    if g % 2 == 0:
                        dve.wait_ge(p1_done, 2 * b + 1 + half)
                        at(dve, av_done, 2 * b - 3 + half)
                    hs = slice(g * GH, (g + 1) * GH)
                    nc.vector.tensor_tensor(p2[:, v, hs, :], p32[:, v, hs, :], p1[:, v, hs, :],
                                            ALU.subtract).then_inc(p2_done, 1)

                def maxima(g):
                    b = k - 1
                    dve.wait_ge(s_done, 4 * b + 1 + g)
                    if g == 0:
                        at(dve, st_done, 2 * b - 2)
                    nc.vector.tensor_reduce(
                        mx[:, 1 - u, g * GH:(g + 1) * GH],
                        s_ps[:, 0:GW].rearrange("p (h k) -> p h k", h=GH), AX.X, ALU.max).then_inc(max_done, 1)

                if has(k, 6):
                    b = k - 6
                    dve.wait_ge(bn2_done, b + 1)
                    at(dve, norm2_ready, 4 * b - 4)
                    nc.vector.sem_inc(dve_passed)
                    nc.vector.bn_aggr(moments[:, u, :], stats[:, :]).then_inc(stat2_done, 1)
                if has(k, 5):
                    b = k - 5
                    dve.wait_ge(proj_done, b + 1)
                    dve.wait_ge(xbo_done, b + 1)
                    nc.vector.tensor_tensor(xs[:, b, :], small_ps[:, 0:D], xs[:, b, :], ALU.add).then_inc(x2_done, 1)
                if has(k, 4):
                    b = k - 4
                    dve.wait_ge(av_done, 2 * b + 2)
                    at(dve, cc_done, b - 1)
                    nc.vector.tensor_reduce(osum[:, u], av_ps[:, 0:HEADS * VW].rearrange(
                        "p (h s c) -> p h c s", h=HEADS, s=3), AX.X, ALU.add).then_inc(osum_done, 1)
                if has(k, 3):
                    low_part(0)
                    low_part(1)
                if has(k, 0):
                    dve.wait_ge(kh_done, k + 1)
                    rows = kst[64:96, u]
                    nc.vector.tensor_tensor(rows, misc_ps[64:96, 0:NG * KV].rearrange("p (g k) -> p g k", g=NG),
                                            rows.bitcast(F32), ALU.subtract).then_inc(k_done, 1)
                if has(k, 1):
                    maxima(0)
                if has(k, 3):
                    low_part(2)
                if has(k, 8):
                    b = k - 8
                    dve.wait_ge(gate_done, b + 1)
                    if isinstance(b, int) and b == 0:
                        dve.wait_ge(wg_in, 32)
                    nc.vector.tensor_tensor(logits[:, b, :], av_ps[:, O_GATE:O_GATE + E], bg_rows[:, :],
                                            ALU.add).then_inc(logit_done, 1)
                if has(k, 4):
                    dve.wait_ge(osum_done, k - 3)
                    nc.vector.reciprocal(rden[:, u, :], osum[:, u, :, DK]).then_inc(rden_done, 1)
                if has(k, 1):
                    maxima(1)
                if has(k, 4):
                    b = k - 4
                    dve.wait_ge(rden_done, b + 1)
                    at(dve, ccT_ps, b - 1)
                    nc.vector.tensor_tensor(
                        cc[:, u, :].rearrange("p (h c) -> p h c", c=DK), osum[:, u, :, 0:DK],
                        rden[:, u, :].unsqueeze(2).broadcast_to([T, HEADS, DK]), ALU.mult).then_inc(cc_done, 1)
                if has(k, 3):
                    low_part(3)
                if has(k, 1):
                    maxima(2)
                if has(k, 0):
                    dve.wait_ge(q_ps, k + 1)
                    at(dve, q_done, k)
                    nc.vector.tensor_tensor(qb[:, :, :], misc_ps[0:ROWS, :].rearrange("p (g t) -> p g t", g=NG),
                                            bq3[:, :].unsqueeze(2).broadcast_to([ROWS, NG, T]),
                                            ALU.add).then_inc(qb_done, 1)
                if has(k, 5):
                    b = k - 5
                    dve.wait_ge(x2_done, b + 1)
                    at(dve, stat2_done, b)
                    nc.vector.sem_inc(dve_passed)
                    nc.vector.bn_stats(stats[:, :], xs[:, b, :]).then_inc(bn2_done, 1)
                if has(k, 1):
                    maxima(3)

            steps(dve, step)

            made = [0]

            def link(instruction):
                made[0] += 1
                instruction.then_inc(chain, 1)
                dve.wait_ge(chain, made[0])

            dve.wait_ge(logit_done, B)
            link(nc.vector.tensor_reduce(row_stat[:, :], logits[:, :, :], AX.X, ALU.max))
            nc.vector.tensor_tensor(logits[:, :, :], logits[:, :, :],
                                    row_stat[:, :].unsqueeze(2).broadcast_to([T, B, E]),
                                    ALU.subtract).then_inc(logits_done, 1)
            dve.wait_ge(gate_exp, 1)
            link(nc.vector.tensor_reduce(row_stat[:, :], probs[:, :, :], AX.X, ALU.add))
            link(nc.vector.reciprocal(row_stat[:, :], row_stat[:, :]))
            link(nc.vector.tensor_tensor(probs[:, :, :], probs[:, :, :],
                                         row_stat[:, :].unsqueeze(2).broadcast_to([T, B, E]), ALU.mult))
            for c in range(2):
                pick = onehot[:, :, c, :]
                link(nc.vector.tensor_reduce(top[:, :, c], probs[:, :, :], AX.X, ALU.max))
                link(nc.vector.tensor_tensor(pick, probs[:, :, :], top[:, :, c].unsqueeze(2).broadcast_to([T, B, E]),
                                             ALU.is_equal))
                link(nc.vector.tensor_tensor(pick, pick, rank_e[:, :].unsqueeze(1).broadcast_to([T, B, E]), ALU.mult))
                link(nc.vector.tensor_reduce(row_stat[:, :], pick, AX.X, ALU.max))
                link(nc.vector.tensor_tensor(pick, pick, row_stat[:, :].unsqueeze(2).broadcast_to([T, B, E]),
                                             ALU.is_equal))
                if c == 0:
                    link(nc.vector.scalar_tensor_tensor(out=probs[:, :, :], in0=pick, scalar=-2.0, in1=probs[:, :, :],
                                                        op0=ALU.mult, op1=ALU.add))
            nc.vector.tensor_tensor(chosen[:, :, :], onehot[:, :, 0, :], onehot[:, :, 1, :],
                                    ALU.add).then_inc(chosen_done, 1)
            dve.wait_ge(count_done, 2)
            link(nc.vector.tensor_copy(scan[:, 0], pair_ps[:, 0, :].rearrange("p (b e) -> p b e", e=E)))
            a = 0
            step_ = 1
            while step_ < B:
                nc.vector.tensor_copy(scan[:, 1 - a, 0:step_, :], scan[:, a, 0:step_, :]).then_inc(chain, 1)
                made[0] += 1
                link(nc.vector.tensor_tensor(scan[:, 1 - a, step_:B, :], scan[:, a, step_:B, :],
                                             scan[:, a, 0:B - step_, :], ALU.add))
                a = 1 - a
                step_ *= 2
            total = scan[:, a, B - 1, :]
            link(nc.vector.tensor_scalar(ntile[:, :], total, float(TILE - 1), None, ALU.add))
            link(nc.vector.tensor_copy(ntile_i[:, :], ntile[:, :]))
            link(nc.vector.tensor_scalar(ntile_i[:, :], ntile_i[:, :], TILE.bit_length() - 1, None,
                                         ALU.arith_shift_right))
            link(nc.vector.tensor_copy(ntile[:, :], ntile_i[:, :]))
            link(nc.vector.tensor_copy(cum[:, 0, :], ntile[:, :]))
            c = 0
            step_ = 1
            while step_ < E:
                nc.vector.tensor_copy(cum[:, 1 - c, 0:step_], cum[:, c, 0:step_]).then_inc(chain, 1)
                made[0] += 1
                link(nc.vector.tensor_tensor(cum[:, 1 - c, step_:E], cum[:, c, step_:E], cum[:, c, 0:E - step_],
                                             ALU.add))
                c = 1 - c
                step_ *= 2
            link(nc.vector.tensor_tensor(first_row[:, :], cum[:, c, :], ntile[:, :], ALU.subtract))
            link(nc.vector.tensor_scalar(first_row[:, :], first_row[:, :], float(TILE), None, ALU.mult))
            link(nc.vector.tensor_tensor(place[:, :, :], scan[:, a], pair_ps[:, 0, :].rearrange("p (b e) -> p b e", e=E),
                                         ALU.subtract))
            link(nc.vector.tensor_tensor(place[:, :, :], place[:, :, :],
                                         pair_ps[:, 1, :].rearrange("p (b e) -> p b e", e=E), ALU.add))
            link(nc.vector.tensor_tensor(place[:, :, :], place[:, :, :],
                                         first_row[:, :].unsqueeze(1).broadcast_to([T, B, E]), ALU.add))
            link(nc.vector.tensor_tensor(onehot[:, :, :, :], onehot[:, :, :, :],
                                         place[:, :, :].unsqueeze(2).broadcast_to([T, B, 2, E]), ALU.mult))
            link(nc.vector.tensor_reduce(slot_f[:, :, :], onehot[:, :, :, :], AX.X, ALU.add))
            link(nc.vector.tensor_copy(slots[:, :, :], slot_f[:, :, :]))
            def dispatch(b, u):
                if not isinstance(b, int):
                    dve.wait_ge(scattered[u], (b - u) * (32 // ROWS_DEEP))
                nc.vector.tensor_scalar(nrow[:, u, :, 0:D], xs[:, b, :].unsqueeze(1).broadcast_to([T, 2, D]),
                                        rstd[:, bass.ds(b, 1)], shift[:, bass.ds(b, 1)],
                                        ALU.mult, ALU.add).then_inc(row_done, 1)
                nc.vector.tensor_copy(nrow[:, u, :, D].bitcast(I32), result_row[:, b, :]).then_inc(row_done, 1)
                nc.vector.tensor_copy(slot_now[:, u, :], slots[:, b, :]).then_inc(row_done, 1)

            for u in range(ROWS_DEEP):
                dispatch(u, u)
            with dve.Fori(0, B // ROWS_DEEP - 1) as i:
                for u in range(ROWS_DEEP):
                    dispatch(i * ROWS_DEEP + (u + ROWS_DEEP), u)

            link(nc.vector.tensor_tensor(reached[:, :, :],
                                         tile_no[:, :].unsqueeze(2).broadcast_to([1, TILES, E - 1]),
                                         cum[0:1, c, 0:E - 1].unsqueeze(1).broadcast_to([1, TILES, E - 1]), ALU.is_ge))
            link(nc.vector.tensor_reduce(tile_f[:, :], reached[:, :, :], AX.X, ALU.add))
            nc.vector.tensor_copy(tile_expert[:, :], tile_f[:, :]).then_inc(table_done, 1)

            link(nc.vector.tensor_tensor(row_stat[:, :], top[:, :, 0], top[:, :, 1], ALU.add))
            link(nc.vector.tensor_scalar(row_stat[:, :], row_stat[:, :], 1e-8, None, ALU.add))
            link(nc.vector.reciprocal(row_stat[:, :], row_stat[:, :]))
            link(nc.vector.tensor_tensor(weight[:, :, :], top[:, :, 0:2],
                                         row_stat[:, :].unsqueeze(2).broadcast_to([T, B, 2]), ALU.mult))
            link(nc.vector.tensor_scalar(weight[:, :, :], weight[:, :, :], gate[:, 1:2], None, ALU.mult))

            dve.wait_ge(table_done, 1)
            dve.wait_ge(experts_in, 16 * (3 + 2 * FC))
            dve.wait_ge(w1_split, 1)
            low = w1_low.rearrange("p (e f) -> p e f", e=E)
            nc.vector.tensor_tensor(low.bitcast(F32R), low, experts[:, :, 0:F], ALU.subtract).then_inc(w1_split, 1)
            dve.wait_ge(w1_split, 2)

            def tile_step(k, u):
                if has_tile(k, 0):
                    idx = tile_expert[0:1, k:k + 1] if isinstance(k, int) else tile_expert[0:1, bass.ds(k, 1)]
                    e = dve.value_load(idx, min_val=0, max_val=E - 1)
                    if has_tile(k, 2):
                        dve.wait_ge(h_ps, k - 1)
                    nc.vector.tensor_copy(w1_now[:, u, :],
                                          arena[:, bass.ds(e * BUNDLE, F)].bitcast(F32R)).then_inc(w1_done, 1)
                    nc.vector.tensor_copy(w1_low_now[:, u, :],
                                          arena[:, bass.ds(e * F + E * BUNDLE, F)].bitcast(F32R)).then_inc(w1_done, 1)
                    dve.wait_ge(xgT_high, k + 1)
                    nc.vector.tensor_tensor(xgT_low[:, u, :], misc_ps[:, 0:TILE], xgT[:, u, :].bitcast(F32),
                                            ALU.subtract).then_inc(xgT_sb, 1)
                if has_tile(k, 2):
                    if has_tile(k, 4):
                        dve.wait_ge(y_out[u], (k - u) * 8 * SUB - 16 * SUB)
                    dve.wait_ge(row_first_done, k - 1)
                    nc.vector.tensor_copy(row_now[:, u, :], row_first[:, u, :]).then_inc(row_now_done, 1)
                    dve.wait_ge(y_ps, k - 1)
                    nc.vector.tensor_tensor(yb[:, u], pair_ps[:, u, 0:TILE].rearrange("p (s d) -> p s d", s=SUB),
                                            wbuf[:, u, O_B2:BUNDLE].unsqueeze(1).broadcast_to([128, SUB, D]), ALU.add).then_inc(y_done, 1)
                if has_tile(k, 0):
                    if has_tile(k, 2):
                        dve.wait_ge(row_now_done, k - 1)
                    nc.vector.tensor_copy(row_first[:, u, :], xg[:, u, :, D].bitcast(I32)).then_inc(row_first_done, 1)
                    if has_tile(k, 2):
                        dve.wait_ge(y_done, k - 1)
                    nc.vector.tensor_copy(wbuf[:, u, F:BUNDLE],
                                          arena[:, bass.ds(e * BUNDLE + F, BUNDLE - F)]).then_inc(w2_done, 1)

            for u in range(ROWS_DEEP):
                dve.wait_ge(scattered[u], 32 * (B // ROWS_DEEP))
            tile_steps(dve, tile_step)

            with dve.Fori(0, B // RB // PICKS) as i:
                for u in range(PICKS):
                    c = i * PICKS + u
                    dve.wait_ge(picked_in[u], i * 16 + 16)
                    for w in range(2):
                        done = res_chain if w == 0 else res_done
                        for j in range(RB):
                            b = c * RB + j
                            if w == 1:
                                dve.wait_ge(res_chain, b + 1)
                            nc.vector.scalar_tensor_tensor(
                                out=xs[:, b, :], in0=picked[:, u, j, w * D:(w + 1) * D], scalar=weight[:, b, w:w + 1],
                                in1=xs[:, b, :], op0=ALU.mult, op1=ALU.add).then_inc(done, 1)

        @block.tensor
        def _(pe):
            def turn(c, u):
                pe.wait_ge(ctx_in_u[u], (c // 2) * 16 + 16 if isinstance(c, int) else (c - u) * 8 + 16)
                if not isinstance(c, int) or c >= 2:
                    pe.wait_ge(ctxT_sb, 2 * c - 2)
                dst = misc_ps if u == 0 else av_ps
                for j in range(CB):
                    last = nc.tensor.transpose(dst[0:DC + 1, j * KV:(j + 1) * KV], ctx_rows[:, u, j, :],
                                               ident[0:KV, 0:KV])
                last.then_inc(ctxT_ps, 1)

            def values(c, u):
                pe.wait_ge(ctxT_sb, c * 2 + 1)
                if not isinstance(c, int) or c >= 2:
                    pe.wait_ge(v_chain, c * 3 - 5)
                for j in range(CB):
                    last = nc.tensor.matmul(st_ps[0:KV, u, 0, j * D:(j + 1) * D],
                                            ctxT_now[:, u, j * KV:(j + 1) * KV], wv[:, :], start=True, stop=True)
                last.then_inc(v_ps, 1)

            pe.wait_ge(const_made, VALUES_CLEAR)
            for u in range(2):
                turn(u, u)
            pe.wait_ge(wv_in, 32)
            values(0, 0)
            turn(2, 0)
            values(1, 1)
            turn(3, 1)
            values(2, 0)
            with pe.Fori(0, B // CB // 2 - 2) as i:
                for u in range(2):
                    c = i * 2 + (u + 4)
                    turn(c, u)
                    values(c - 1, 1 - u)
            values(B // CB - 1, 1)

            def step(k, u):
                def scores_t(half):
                    b = k - 2
                    if half == 0:
                        pe.wait_ge(max_done, 4 * b + 4)
                    at(pe, p1_done, 2 * b - 1 + half)
                    for n in range(HALF):
                        h = half * HALF + n
                        dst = st_ps[0:KV, half, n // GH, (n % GH) * T:(n % GH + 1) * T]
                        nc.tensor.matmul(dst, km[:, u, h // GH, h % GH, :], qst[:, u, h // GH, :],
                                         start=True, stop=False)
                        last = nc.tensor.matmul(dst, mx[:, u, h:h + 1].broadcast_to([T, KV]), neg_ident[:, :],
                                                start=False, stop=True)
                    last.then_inc(st_done, 1)

                def scores(g, lag):
                    b = k - lag
                    v = (u + lag) % 2
                    if g == 0:
                        pe.wait_ge(q_done, b + 1)
                    at(pe, max_done, 4 * b + g)
                    nc.tensor.matmul(s_ps[:, 0:GW], qst[:, v, g, :],
                                     km[:, v, g].rearrange("p h k -> p (h k)"),
                                     start=True, stop=True).then_inc(s_done, 1)

                def weighted(half):
                    b = k - 4
                    if half == 0:
                        pe.wait_ge(v_in[u], (b - u) * 8 + 16)
                    if half == 0 and has(k - 1, 8):
                        pe.wait_ge(logit_done, k - 8)
                    else:
                        if half == 0:
                            at(pe, osum_done, b)
                        pe.wait_ge(p2_done, 4 * b + 2 + 2 * half)
                    for h in range(half * HALF, (half + 1) * HALF):
                        nc.tensor.matmul(av_ps[:, h * VW:(h + 1) * VW], p1[:, u, h, :],
                                         v_now[:, u, h * VW:(h + 1) * VW], start=True, stop=False)
                        last = nc.tensor.matmul(av_ps[:, h * VW + DK + 1:(h + 1) * VW], p2[:, u, h, :],
                                                v_now[:, u, h * VW:h * VW + 2 * DK + 2], start=False, stop=True)
                    last.then_inc(av_done, 1)

                if has(k, 2):
                    scores(2, 2)
                if has(k, 4):
                    weighted(0)
                if has(k, 5):
                    pe.wait_ge(cc_done, k - 4)
                    bank_free(pe, k, SMALL_USERS, CCT)
                    nc.tensor.transpose(small_ps[:, 0:T], cc[:, 1 - u, :], ident[:, :]).then_inc(ccT_ps, 1)
                if has(k, 4):
                    weighted(1)
                if has(k, 2):
                    scores(3, 2)
                if has(k, 5):
                    bank_free(pe, k, SMALL_USERS, PROJ)
                    nc.tensor.matmul(small_ps[:, 0:D], ccT[:, 1 - u, :], wo[:, :], start=True, stop=True).then_inc(proj_done, 1)
                if has(k, 0):
                    bank_free(pe, k, MISC_USERS, KEYS)
                    for g in range(NG):
                        last = nc.tensor.matmul(misc_ps[0:ROWS, g * KV:(g + 1) * KV], wk3[:, g, :],
                                                ctxT[:, bass.ds(k * KV, KV)], start=True, stop=True)
                    last.then_inc(k_ps, 1)
                if has(k, 2):
                    scores_t(0)
                if has(k, 0):
                    pe.wait_ge(xn_done, k + 1)
                    bank_free(pe, k, SMALL_USERS, XNT)
                    nc.tensor.transpose(small_ps[:, 0:T], xn[:, u, :], ident[:, :]).then_inc(xnT_ps, 1)
                if has(k, 1):
                    scores(0, 1)
                if has(k, 2):
                    scores_t(1)
                if has(k, 1):
                    scores(1, 1)
                if has(k, 8):
                    b = k - 8
                    pe.wait_ge(xn2T_sb, b + 1)
                    if not has(k, 1):
                        pe.wait_ge(osum_done, min(k - 3, B))
                    if isinstance(b, int) and b == 0:
                        pe.wait_ge(wg_in, 32)
                    elif not has(k, 4):
                        pe.wait_ge(logit_done, b)
                    nc.tensor.matmul(av_ps[:, O_GATE:O_GATE + E], xn2T[:, u, :], wg[:, :],
                                     start=True, stop=True).then_inc(gate_done, 1)
                if has(k, 7):
                    pe.wait_ge(xn2_done, k - 6)
                    if not has(k, 0):
                        bank_free(pe, k, SMALL_USERS, XN2T)
                    nc.tensor.transpose(small_ps[:, 0:T], xn2[:, 1 - u, :], ident[:, :]).then_inc(xn2T_ps, 1)
                if has(k, 0):
                    if not has(k, 7):
                        pe.wait_ge(xnT_sb, k + 1)
                    bank_free(pe, k, MISC_USERS, QUERIES)
                    for g in range(NG):
                        last = nc.tensor.matmul(misc_ps[0:ROWS, g * T:(g + 1) * T], wq3[:, g, :], xnT[:, u, :],
                                                start=True, stop=True)
                    last.then_inc(q_ps, 1)

            pe.wait_ge(const_made, ALL_CONSTS)
            pe.wait_ge(weights_in, WEIGHT_LOADS)
            pe.wait_ge(wo_scaled, 2)
            pe.wait_ge(ctxT_sb, 2 * (B // CB))
            pe.wait_ge(v_chain, 3 * (B // CB) - 2)
            steps(pe, step)

            pe.wait_ge(chosen_done, 1)
            pe.wait_ge(max_done, 4 * B)
            rows = chosen[:, :, :].rearrange("p b e -> p (b e)")
            nc.tensor.matmul(pair_ps[:, 0, :], ones[:, :], rows, start=True, stop=True).then_inc(count_done, 1)
            nc.tensor.matmul(pair_ps[:, 1, :], before[:, :], rows, start=True, stop=True).then_inc(count_done, 1)

            def tile_step(k, u):
                if has_tile(k, 0):
                    pe.wait_ge(xg_in[u], (k // 2) * 16 + 16 if isinstance(k, int) else (k - u) * 8 + 16)
                    at(pe, xgT_sb, k)
                    for s_ in range(SUB):
                        last = nc.tensor.transpose(misc_ps[:, s_ * 128:(s_ + 1) * 128], xg[:, u, s_, 0:D], ident[:, :])
                    last.then_inc(xgT_ps, 1)
                if has_tile(k, 1):
                    v = 1 - u
                    pe.wait_ge(xgT_sb, k)
                    pe.wait_ge(w1_done, 2 * k)
                    if has_tile(k, 3):
                        pe.wait_ge(h_sb, (k - 2) * FC)
                    for c in range(FC):
                        dst = st_ps[:, v, c // 2, (c % 2) * TILE:(c % 2 + 1) * TILE]
                        high = w1_now[:, v, c * 128:(c + 1) * 128]
                        low = w1_low_now[:, v, c * 128:(c + 1) * 128]
                        nc.tensor.matmul(dst, high, xgT[:, v, :], start=True, stop=False)
                        nc.tensor.matmul(dst, low, xgT[:, v, :], start=False, stop=False)
                        last = nc.tensor.matmul(dst, high, xgT_low[:, v, :], start=False, stop=True)
                    last.then_inc(h_ps, 1)
                if has_tile(k, 2):
                    pe.wait_ge(h_sb, (k - 1) * FC)
                    pe.wait_ge(w2_done, k - 1)
                    if has_tile(k, 4):
                        pe.wait_ge(y_done, k - 3)
                    for s_ in range(SUB):
                        for c in range(FC):
                            last = nc.tensor.matmul(pair_ps[:, u, s_ * D:(s_ + 1) * D],
                                                    hT[:, u, c, s_ * 128:(s_ + 1) * 128],
                                                    wbuf[:, u, O_W2 + c * D:O_W2 + (c + 1) * D],
                                                    start=(c == 0), stop=(c == FC - 1))
                    last.then_inc(y_ps, 1)

            pe.wait_ge(table_done, 1)
            tile_steps(pe, tile_step)


_INS = ['x', 'ctx_512', 'g_xattn', 'g_ffn', 'L0_xattn_Wq', 'L0_xattn_bq', 'L0_xattn_Wk', 'L0_xattn_bk', 'L0_xattn_Wv',
        'L0_xattn_bv', 'L0_xattn_Wo', 'L0_xattn_bo', 'L0_ffn_Wg', 'L0_ffn_bg', 'L0_ffn_W1', 'L0_ffn_b1', 'L0_ffn_W2',
        'L0_ffn_b2']


def kernel(**inputs):
    import numpy as _np
    import concourse.bacc as _bacc
    from concourse import mybir as _mybir
    from concourse.bass_utils import run_bass_kernel_spmd as _run

    nc = _bacc.Bacc("TRN2", target_bir_lowering=False, num_devices=1)
    arrays, args = {}, []
    for name in _INS:
        a = _np.ascontiguousarray(inputs[name])
        arrays[f"in_{name}"] = a
        args.append(nc.dram_tensor(f"in_{name}", a.shape, _mybir.dt.from_np(a.dtype), kind="ExternalInput").ap())
    shape = inputs["x"].shape
    args.append(nc.dram_tensor("out_x", shape, _mybir.dt.float32, kind="ExternalOutput").ap())
    flamingo(nc, *args)
    return _run(nc, [arrays], core_ids=[0]).results[0]["out_x"]
```
